# Optimizing a Trainium2 kernel written in Bass

```python
import numpy as np
import jax
import jax.numpy as jnp

def _softmax(x, axis=-1):
    return jax.nn.softmax(x, axis=axis)

def _gelu(x):
    return jax.nn.gelu(x, approximate=True)

def _silu(x):
    return jax.nn.silu(x)

def _sigmoid(x):
    return jax.nn.sigmoid(x)

def _layernorm(x, axis=-1, eps=1e-05):
    m = jnp.mean(x, axis=axis, keepdims=True)
    v = jnp.var(x, axis=axis, keepdims=True)
    return (x - m) / jnp.sqrt(v + eps)

def _scatter_add(tgt, idx, src, axis=0):
    return tgt.at[idx].add(src)

def _segment_sum(src, seg, n):
    return jax.ops.segment_sum(src, seg, n)
kernel_name = 'mk_cond_seq_d2_seqx_r2_41c9fc'

def setup_inputs(seed: int=0):
    np.random.seed(seed)
    _w = jnp.asarray

    def _rec_inputs():
        import jax
        import jax.numpy as jnp
        _rk = jax.random.key(seed)
        x = -0.000125 + 0.9999 * jax.random.normal(jax.random.fold_in(_rk, 1), (2, 2048, 512), jnp.float32)
        _lenS = 2048 - jax.random.randint(jax.random.fold_in(_rk, 7), (2,), 0, max(1, 2048 // 4) + 1, jnp.int32)
        _lenS2 = 2048 - jax.random.randint(jax.random.fold_in(_rk, 8), (2,), 0, max(1, 2048 // 4) + 1, jnp.int32)
        itok_B_0_15 = jax.random.randint(jax.random.fold_in(_rk, 11), (2,), 0, 16, jnp.int32)
        condB_gatescore = jax.random.uniform(jax.random.fold_in(_rk, 12), (2,), jnp.float32, 0.0, 0.581427)
        return (x, itok_B_0_15, condB_gatescore)
    x, itok_B_0_15, condB_gatescore = _rec_inputs()

    def _L0_cond_setup():
        import jax, jax.numpy as jnp
        import numpy as np
        B, S, D = (32, 512, 512)
        A = 128
        E = 16
        LN_EPS = 1e-05
        key = jax.random.key(seed)
        ks = jax.random.split(key, 10)
        s = lambda fan_in: 1.0 / np.sqrt(fan_in)
        return {'hidden_states': jax.random.normal(ks[0], (B, S, D), dtype=jnp.float32), 'domain_id': jax.random.randint(ks[1], (B,), 0, E, dtype=jnp.int64), 'down_W': jax.random.uniform(ks[2], (A, D), jnp.float32, -s(D), s(D)), 'down_b': jax.random.uniform(ks[3], (A,), jnp.float32, -s(D), s(D)), 'up_W': jax.random.uniform(ks[4], (D, A), jnp.float32, -s(A), s(A)), 'up_b': jax.random.uniform(ks[5], (D,), jnp.float32, -s(A), s(A)), 'expert_W': jax.random.uniform(ks[6], (E, A, A), jnp.float32, -s(A), s(A)), 'expert_b': jax.random.uniform(ks[7], (E, A), jnp.float32, -s(A), s(A)), 'domain_emb': jax.random.normal(ks[8], (E, A), dtype=jnp.float32), 'ln_gamma': jnp.ones((D,), jnp.float32), 'ln_beta': jnp.zeros((D,), jnp.float32)}
    _L0_cond_all = _L0_cond_setup()
    _L0_cond_in = {k: v for k, v in _L0_cond_all.items() if k in ('down_W', 'down_b', 'up_W', 'up_b', 'expert_W', 'expert_b', 'domain_emb', 'ln_gamma', 'ln_beta')}
    del _L0_cond_all

    def _L1_cond_setup():
        import jax, jax.numpy as jnp
        import numpy as np
        D_MODEL = 512
        N_HEADS = 16
        D_HEAD = D_MODEL // N_HEADS
        D_FF = 2048
        EPS = 1e-05

        def layernorm(x, gamma, beta):
            mu = jnp.mean(x, axis=-1, keepdims=True)
            var = jnp.var(x, axis=-1, keepdims=True)
            return (x - mu) * jax.lax.rsqrt(var + EPS) * gamma + beta
        key = jax.random.key(seed)
        ks = jax.random.split(key, 16)
        B, T = (4, 1024)
        s = 1.0 / np.sqrt(D_MODEL)
        sf = 1.0 / np.sqrt(D_FF)
        return {'x': jax.random.normal(ks[0], (B, T, D_MODEL), jnp.float32), 'gate_score': jax.random.uniform(ks[1], (B,), jnp.float32), 'Wq': jax.random.normal(ks[2], (D_MODEL, D_MODEL), jnp.float32) * s, 'bq': jnp.zeros((D_MODEL,), jnp.float32), 'Wk': jax.random.normal(ks[3], (D_MODEL, D_MODEL), jnp.float32) * s, 'bk': jnp.zeros((D_MODEL,), jnp.float32), 'Wv': jax.random.normal(ks[4], (D_MODEL, D_MODEL), jnp.float32) * s, 'bv': jnp.zeros((D_MODEL,), jnp.float32), 'Wo': jax.random.normal(ks[5], (D_MODEL, D_MODEL), jnp.float32) * s, 'bo': jnp.zeros((D_MODEL,), jnp.float32), 'W1': jax.random.normal(ks[6], (D_MODEL, D_FF), jnp.float32) * s, 'b1': jnp.zeros((D_FF,), jnp.float32), 'W2': jax.random.normal(ks[7], (D_FF, D_MODEL), jnp.float32) * sf, 'b2': jnp.zeros((D_MODEL,), jnp.float32), 'gamma1': jnp.ones((D_MODEL,), jnp.float32), 'beta1': jnp.zeros((D_MODEL,), jnp.float32), 'gamma2': jnp.ones((D_MODEL,), jnp.float32), 'beta2': jnp.zeros((D_MODEL,), jnp.float32)}
    _L1_cond_all = _L1_cond_setup()
    _L1_cond_in = {k: v for k, v in _L1_cond_all.items() if k in ('Wq', 'bq', 'Wk', 'bk', 'Wv', 'bv', 'Wo', 'bo', 'W1', 'b1', 'W2', 'b2', 'gamma1', 'beta1', 'gamma2', 'beta2')}
    del _L1_cond_all
    return {'x': x, 'itok_B_0_15': itok_B_0_15, 'condB_gatescore': condB_gatescore, 'L0_cond_down_W': _L0_cond_in['down_W'], 'L0_cond_down_b': _L0_cond_in['down_b'], 'L0_cond_up_W': _L0_cond_in['up_W'], 'L0_cond_up_b': _L0_cond_in['up_b'], 'L0_cond_expert_W': _L0_cond_in['expert_W'], 'L0_cond_expert_b': _L0_cond_in['expert_b'], 'L0_cond_domain_emb': _L0_cond_in['domain_emb'], 'L0_cond_ln_gamma': _L0_cond_in['ln_gamma'], 'L0_cond_ln_beta': _L0_cond_in['ln_beta'], 'L1_cond_Wq': _L1_cond_in['Wq'], 'L1_cond_bq': _L1_cond_in['bq'], 'L1_cond_Wk': _L1_cond_in['Wk'], 'L1_cond_bk': _L1_cond_in['bk'], 'L1_cond_Wv': _L1_cond_in['Wv'], 'L1_cond_bv': _L1_cond_in['bv'], 'L1_cond_Wo': _L1_cond_in['Wo'], 'L1_cond_bo': _L1_cond_in['bo'], 'L1_cond_W1': _L1_cond_in['W1'], 'L1_cond_b1': _L1_cond_in['b1'], 'L1_cond_W2': _L1_cond_in['W2'], 'L1_cond_b2': _L1_cond_in['b2'], 'L1_cond_gamma1': _L1_cond_in['gamma1'], 'L1_cond_beta1': _L1_cond_in['beta1'], 'L1_cond_gamma2': _L1_cond_in['gamma2'], 'L1_cond_beta2': _L1_cond_in['beta2']}

def reference(x, itok_B_0_15, condB_gatescore, L0_cond_down_W, L0_cond_down_b, L0_cond_up_W, L0_cond_up_b, L0_cond_expert_W, L0_cond_expert_b, L0_cond_domain_emb, L0_cond_ln_gamma, L0_cond_ln_beta, L1_cond_Wq, L1_cond_bq, L1_cond_Wk, L1_cond_bk, L1_cond_Wv, L1_cond_bv, L1_cond_Wo, L1_cond_bo, L1_cond_W1, L1_cond_b1, L1_cond_W2, L1_cond_b2, L1_cond_gamma1, L1_cond_beta1, L1_cond_gamma2, L1_cond_beta2):
    import jax
    import jax.numpy as jnp

    def _L0_cond_ref(hidden_states, domain_id, down_W, down_b, up_W, up_b, expert_W, expert_b, domain_emb, ln_gamma, ln_beta):
        import jax, jax.numpy as jnp
        import numpy as np
        B, S, D = (32, 512, 512)
        A = 128
        E = 16
        LN_EPS = 1e-05
        residual = hidden_states
        hidden = jnp.einsum('bsd,ad->bsa', hidden_states, down_W) + down_b
        hidden = jax.nn.gelu(hidden, approximate=False)
        valid = (domain_id >= 0) & (domain_id < E)
        idx = jnp.clip(domain_id, 0, E - 1)
        Wsel = expert_W[idx]
        bsel = expert_b[idx]
        expert_out = jnp.einsum('bsa,boa->bso', hidden, Wsel) + bsel[:, None, :]
        domain_output = jnp.where(valid[:, None, None], expert_out, hidden)
        hidden = domain_output + domain_emb[idx][:, None, :]
        hidden = jnp.einsum('bsa,da->bsd', hidden, up_W) + up_b
        x = hidden + residual
        mu = jnp.mean(x, axis=-1, keepdims=True)
        var = jnp.mean(jnp.square(x - mu), axis=-1, keepdims=True)
        return (x - mu) * jax.lax.rsqrt(var + LN_EPS) * ln_gamma + ln_beta

    def _L1_cond_ref(x, gate_score, Wq, bq, Wk, bk, Wv, bv, Wo, bo, W1, b1, W2, b2, gamma1, beta1, gamma2, beta2):
        import jax, jax.numpy as jnp
        import numpy as np
        D_MODEL = 512
        N_HEADS = 16
        D_HEAD = D_MODEL // N_HEADS
        D_FF = 2048
        EPS = 1e-05

        def layernorm(x, gamma, beta):
            mu = jnp.mean(x, axis=-1, keepdims=True)
            var = jnp.var(x, axis=-1, keepdims=True)
            return (x - mu) * jax.lax.rsqrt(var + EPS) * gamma + beta
        B, T, C = x.shape
        h = layernorm(x, gamma1, beta1)
        Q = (h @ Wq + bq).reshape(B, T, N_HEADS, D_HEAD).transpose(0, 2, 1, 3)
        K = (h @ Wk + bk).reshape(B, T, N_HEADS, D_HEAD).transpose(0, 2, 1, 3)
        V = (h @ Wv + bv).reshape(B, T, N_HEADS, D_HEAD).transpose(0, 2, 1, 3)
        scores = jnp.einsum('bhqd,bhkd->bhqk', Q, K) / np.sqrt(D_HEAD)
        causal = jnp.tril(jnp.ones((T, T), dtype=bool))
        scores = jnp.where(causal, scores, -jnp.inf)
        attn = jax.nn.softmax(scores, axis=-1)
        ctx = jnp.einsum('bhqk,bhkd->bhqd', attn, V)
        ctx = ctx.transpose(0, 2, 1, 3).reshape(B, T, C)
        attn_out = ctx @ Wo + bo
        x1 = x + attn_out
        h2 = layernorm(x1, gamma2, beta2)
        ff = jax.nn.gelu(h2 @ W1 + b1, approximate=False) @ W2 + b2
        x2 = x1 + ff
        g = gate_score[:, None, None]
        return x + g * (x2 - x)
    x = _L0_cond_ref(x, itok_B_0_15, L0_cond_down_W, L0_cond_down_b, L0_cond_up_W, L0_cond_up_b, L0_cond_expert_W, L0_cond_expert_b, L0_cond_domain_emb, L0_cond_ln_gamma, L0_cond_ln_beta)
    x = _L1_cond_ref(x, condB_gatescore, L1_cond_Wq, L1_cond_bq, L1_cond_Wk, L1_cond_bk, L1_cond_Wv, L1_cond_bv, L1_cond_Wo, L1_cond_bo, L1_cond_W1, L1_cond_b1, L1_cond_W2, L1_cond_b2, L1_cond_gamma1, L1_cond_beta1, L1_cond_gamma2, L1_cond_beta2)
    return x

_drawn_inputs = setup_inputs


def setup_inputs(seed=0):
    import zlib

    import numpy as np

    out = dict(_drawn_inputs(seed))
    spreads = {'L0_cond_ln_gamma': (1.0, 0.2),
     'L0_cond_ln_beta': (0.0, 0.1),
     'L1_cond_bq': (0.0, 0.8),
     'L1_cond_bk': (0.0, 0.8),
     'L1_cond_bv': (0.0, 0.327),
     'L1_cond_bo': (0.0, 0.309),
     'L1_cond_b1': (0.0, 0.543),
     'L1_cond_b2': (0.0, 0.367),
     'L1_cond_gamma1': (1.0, 0.6),
     'L1_cond_beta1': (0.0, 0.289),
     'L1_cond_gamma2': (1.0, 0.2),
     'L1_cond_beta2': (0.0, 0.538)}
    factors = {'L0_cond_down_b': 8.0, 'L1_cond_Wq': 3.303, 'L1_cond_Wk': 3.245}
    for name, (base, spread) in spreads.items():
        noise = np.random.default_rng([zlib.crc32(name.encode()), seed]).standard_normal(out[name].shape)
        drawn = base * np.exp(spread * noise) if base else spread * noise
        out[name] = jnp.asarray(drawn.astype(out[name].dtype))
    for name, factor in factors.items():
        out[name] = (out[name] * factor).astype(out[name].dtype)
    return out
```

```python
from contextlib import ExitStack

import concourse.bass as bass
from concourse import mybir

F32 = mybir.dt.float32
BF16 = mybir.dt.bfloat16
F32R = mybir.dt.float32r
I32 = mybir.dt.int32
ACT = mybir.ActivationFunctionType
ALU = mybir.AluOpType
AX = mybir.AxisListType

P = 128
BATCH, SEQ, D = 2, 2048, 512
TOKENS = BATCH * SEQ
KD = D // P
A, EXPERTS = 128, 16
HEADS, DH = 16, 32
F = 2048
KF = F // P
EPS = 1e-5
LOWEST = -3.0e38

C_DOWN_B = 0
C_EXPERT_B = C_DOWN_B + 1
C_EMB = C_EXPERT_B + EXPERTS
C_BQK = C_EMB + EXPERTS
C_G1 = C_BQK + 2 * KD
C_B1LN = C_G1 + KD
C_G2 = C_B1LN + KD
C_B2LN = C_G2 + KD
C_MLP_B1 = C_B2LN + KD
COLS = C_MLP_B1 + KF
R_UP_B, R_LN_G, R_LN_B, R_BV, R_BO, R_B2 = range(6)


def product3(pe, out, left, right, start, stop):
    pe.matmul(out, left[0], right[0], start=start, stop=False)
    pe.matmul(out, left[0], right[1], start=False, stop=False)
    return pe.matmul(out, left[1], right[0], start=False, stop=stop)


def stand_alone(eng, passed):
    eng.sem_inc(passed, 1)


def make_identity(pool, ident, made):
    pool.memset(ident, 0.0).then_inc(made, 1)
    pool.wait_ge(made, 1)
    pool.affine_select(out=ident, in_=ident, compare_op=ALU.not_equal, fill=1.0, base=0,
                       pattern=[[-1, P]], channel_multiplier=1).then_inc(made, 1)


def project(nc, x, xt, down_t, up_t, expert_t, cols, rows, ids, wq, wk, wv, x0_s, qk_s, v_s):
    T = 512
    TT = T // P
    PAIRS = SEQ // T
    RING = 4
    UNITS = 3 * KD
    PREP = 5 + BATCH * (EXPERTS + 6)

    ctx = ExitStack()
    with ctx:
        def sb(name, shape, dt=F32):
            return ctx.enter_context(nc.sbuf_tensor(name, shape, dt))

        def sem(name):
            return ctx.enter_context(nc.semaphore(name))

        stage = [sb(f"stage{i}", [P, KD, T]) for i in range(2)]
        wqkv = [sb("wqkv_hi", [P, 3, KD, D], F32R), sb("wqkv_lo", [P, 3, KD, D], F32R)]
        wdown = [sb("wdown_hi", [P, KD, A], F32R), sb("wdown_lo", [P, KD, A], F32R)]
        wup = [sb("wup_hi", [P, D], F32R), sb("wup_lo", [P, D], F32R)]
        wexp_f = sb("wexp_f", [P, BATCH, A])
        wexp = [sb("wexp_hi", [P, BATCH, A], F32R), sb("wexp_lo", [P, BATCH, A], F32R)]
        col = sb("col_a", [P, COLS])
        row = sb("row_a", [P, 4, D])
        ident = sb("ident_a", [P, P])
        idsi = sb("idsi", [P, BATCH], I32)
        idf = sb("idf", [P, 4, BATCH])
        onehot = sb("onehot", [P, BATCH, EXPERTS])
        esel = sb("esel", [P, BATCH, 2, EXPERTS])
        bexp = sb("bexp", [P, 4, BATCH])
        xn = [sb(f"xn{i}", [P, TT, D]) for i in range(2)]
        xtf = sb("xtf", [P, KD, T])
        xts = [sb("xt_hi", [P, KD, T], F32R), sb("xt_lo", [P, KD, T], F32R)]
        hid = sb("hid", [P, T])
        hids = [sb("hid_hi", [P, T], F32R), sb("hid_lo", [P, T], F32R)]
        doms = [sb("dom_hi", [P, T], F32R), sb("dom_lo", [P, T], F32R)]
        nrm = sb("nrm", [P, TT, D])
        htf = [sb(f"htf{i}", [P, T]) for i in range(2)]
        hts = [[sb(f"ht_hi{i}", [P, KD, T], F32R), sb(f"ht_lo{i}", [P, KD, T], F32R)] for i in range(2)]
        qk_out = [sb(f"qk_out{i}", [P, 2, T], F32R) for i in range(RING)]
        v_out = [sb(f"v_out{i}", [P, D]) for i in range(2)]
        stats = sb("stats_a", [P, 2, TT, 6])
        mean_var = sb("mean_var_a", [P, 2, TT, 2])
        veps = sb("veps_a", [P, 2, TT])
        rstd = sb("rstd_a", [P, 2, TT])
        half = sb("half_a", [P, TT])
        ps_main = [ctx.enter_context(nc.psum_tensor(f"ps_main{i}", [P, T], F32)) for i in range(RING)]
        ps_mid = ctx.enter_context(nc.psum_tensor("ps_mid", [P, T], F32))
        ps_up = [ctx.enter_context(nc.psum_tensor(f"ps_up{i}", [P, D], F32)) for i in range(2)]
        ps_tr = ctx.enter_context(nc.psum_tensor("ps_tr", [P, T], F32))

        small_loaded = sem("small_loaded_a")
        stage_loaded = [sem(f"stage_loaded{i}") for i in range(2)]
        stage_split = sem("stage_split")
        stage_hi = sem("stage_hi")
        prep = sem("prep_a")
        ident_made = sem("ident_made_a")
        passed = sem("passed_a")
        xn_loaded = [sem(f"xn_loaded{i}") for i in range(2)]
        xt_loaded = sem("xt_loaded")
        xt_hi = sem("xt_hi_done")
        xt_split = sem("xt_split")
        down_done = sem("down_done")
        gelu_done = sem("gelu_done_a")
        hid_hi = sem("hid_hi_done")
        hid_split = sem("hid_split")
        expert_done = sem("expert_done")
        dom_hi = sem("dom_hi_done")
        dom_split = sem("dom_split")
        biased = sem("biased_a")
        up_done = sem("up_done")
        y_done = sem("y_done")
        stats_done = sem("stats_done_a")
        aggr_done = sem("aggr_done_a")
        veps_done = sem("veps_done_a")
        rstd_done = sem("rstd_done_a")
        scaled = sem("scaled_a")
        x0_done = sem("x0_done")
        nrm_done = sem("nrm_done_a")
        x0_stored = [sem(f"x0_stored{i}") for i in range(2)]
        tr_done = sem("tr_done_a")
        htf_done = sem("htf_done_a")
        ht_hi = sem("ht_hi_done_a")
        ht_split = sem("ht_split_a")
        main_done = sem("main_done")
        qk_hi = sem("qk_hi_done")
        main_free = sem("main_free")
        qk_stored = [sem(f"qk_stored{i}") for i in range(RING)]
        v_stored = [sem(f"v_stored{i}") for i in range(2)]

        def run(eng, window):
            with eng.Fori(0, PAIRS - 1) as it:
                window(it, 0, True, True)
                window(it, 1, True, True)
            window(PAIRS - 1, 0, True, False)
            window(PAIRS - 1, 1, False, False)

        def after(it, par):
            return (it, 1) if par == 0 else (it + 1, 0)

        def tokens(it, par):
            return bass.ds(it * T + par * SEQ, T)

        block = ctx.enter_context(nc.Block())

        @block.sync
        def _(sp):
            sp.dma_start(col[:, :], cols).then_inc(small_loaded, 16)
            sp.dma_start(idsi[:, :], ids).then_inc(small_loaded, 16)
            sp.dma_start(row[:, :, :], rows[:, 0:4, :]).then_inc(small_loaded, 16)
            sp.dma_start(stage[0][:, :, 0:A], down_t.rearrange("(k p) a -> p k a", p=P)).then_inc(stage_loaded[0], 16)
            sp.dma_start(stage[0][:, :, A:2 * A], up_t.rearrange("a (k n) -> a k n", k=KD)).then_inc(stage_loaded[0], 16)

            def load_xt(it, par):
                sp.dma_start(xtf[:, :, :], xt.rearrange("(k p) t -> p k t", p=P)[:, :, tokens(it, par)])\
                  .then_inc(xt_loaded, 16)

            def load_xn(it, par):
                sp.dma_start(xn[par][:, :, :], x[tokens(it, par), :].rearrange("(t p) d -> p t d", p=P))\
                  .then_inc(xn_loaded[par], 16)

            load_xt(0, 0)
            sp.dma_start(stage[1][:, :, :].rearrange("p k n -> p (k n)"),
                         expert_t.rearrange("a e o -> a (e o)")).then_inc(stage_loaded[1], 16)
            load_xn(0, 0)
            load_xn(0, 1)
            for n, w in enumerate((wq, wk, wv)):
                sp.wait_ge(stage_split, n + 1)
                sp.dma_start(stage[n % 2][:, :, :], w.rearrange("(k p) n -> p k n", p=P)).then_inc(stage_loaded[n % 2], 16)
            sp.wait_ge(xt_split, 1)
            load_xt(0, 1)

            def store_x0(it, par):
                N = 2 * it + par
                sp.wait_ge(x0_done, TT * N + TT)
                sp.dma_start(x0_s[tokens(it, par), :].rearrange("(t p) d -> p t d", p=P), xn[par][:, :, :])\
                  .then_inc(x0_stored[par], 16)

            def window(it, par, ahead, load):
                N = 2 * it + par
                if load:
                    sp.wait_ge(xt_split, N + 2)
                    stand_alone(sp, passed)
                    load_xt(it + 1, par)
                    sp.wait_ge(x0_stored[par], 16 * it + 16)
                    sp.wait_ge(nrm_done, TT * N + TT)
                    load_xn(it + 1, par)

                def store_qk(u):
                    sp.wait_ge(main_free, RING + UNITS * N + u + 1)
                    stand_alone(sp, passed)
                    sp.dma_start(qk_s[u // KD, (u % KD) * P:(u % KD + 1) * P, :, tokens(it, par)],
                                 qk_out[u % RING][:, :, :].bitcast(F32)).then_inc(qk_stored[u % RING], 16)

                def store_v(t):
                    sp.wait_ge(main_free, RING + UNITS * N + 2 * KD + t + 1)
                    sp.dma_start(v_s[bass.ds(it * T + par * SEQ + t * P, P), :], v_out[t % 2][:, :])\
                      .then_inc(v_stored[t % 2], 16)

                for u in range(2 * KD):
                    store_qk(u)
                store_v(0)
                store_v(1)
                if ahead:
                    store_x0(*after(it, par))
                store_v(2)
                store_v(3)

            store_x0(0, 0)
            run(sp, window)
            for par in range(2):
                sp.wait_ge(x0_stored[par], 16 * PAIRS)
                sp.wait_ge(v_stored[par], 16 * 2 * 2 * PAIRS)
            for i in range(RING):
                sp.wait_ge(qk_stored[i], 16 * 2 * 2 * PAIRS)

        @block.gpsimd
        def _(pool):
            make_identity(pool, ident[:, :], ident_made)
            pool.memset(half[:, :], -0.5).then_inc(ident_made, 1)
            pool.wait_ge(ident_made, 3)
            pool.wait_ge(small_loaded, 48)

            def window(it, par, ahead, load):
                if not ahead:
                    return
                it, par = after(it, par)
                M = 2 * it + par
                adapter(it, par, M)

            def adapter(it, par, M):
                pool.wait_ge(xn_loaded[par], 16 * it + 16)
                for t in range(TT):
                    pool.tensor_tensor(xn[par][:, t, :], xn[par][:, t, :], row[:, R_UP_B, :], ALU.add).then_inc(biased, 1)
                for ln in range(2):
                    pool.wait_ge(veps_done, 2 * M + ln + 1)
                    pool.tensor_tensor(rstd[:, ln, :], veps[:, ln, :], half[:, :], ALU.pow).then_inc(rstd_done, 1)

            adapter(0, 0, 0)
            run(pool, window)

        @block.scalar
        def _(act):
            act.wait_ge(small_loaded, 48)

            def gelu(M):
                act.wait_ge(down_done, M + 1)
                act.wait_ge(hid_split, M)
                nc.scalar.activation(hid[:, :], ps_mid[:, :], ACT.Gelu, bias=col[:, C_DOWN_B:C_DOWN_B + 1])\
                  .then_inc(gelu_done, 1)

            def domain_hi(M, par):
                act.wait_ge(expert_done, M + 1)
                act.wait_ge(up_done, TT * M)
                nc.scalar.activation(doms[0][:, :], ps_mid[:, :], ACT.Identity, bias=bexp[:, 2, par:par + 1])\
                  .then_inc(dom_hi, 1)

            def affine(M, first=False):
                for k in range(KD):
                    act.wait_ge(tr_done, KD * M + k + 1)
                    if k >= 2 or not first:
                        act.wait_ge(ht_split, KD * M + k - 1)
                    nc.scalar.activation(htf[k % 2][:, :], ps_tr[:, :], ACT.Identity,
                                         scale=col[:, C_G1 + k:C_G1 + k + 1],
                                         bias=col[:, C_B1LN + k:C_B1LN + k + 1]).then_inc(htf_done, 1)

            def window(it, par, ahead, load):
                N = 2 * it + par

                def qk(u):
                    act.wait_ge(main_done, UNITS * N + u + 1)
                    act.wait_ge(qk_stored[u % RING], 16 * (2 * N + u // RING))
                    nc.scalar.activation(qk_out[u % RING][:, 0, :], ps_main[u % RING][:, :], ACT.Identity,
                                         bias=col[:, C_BQK + u:C_BQK + u + 1]).then_inc(qk_hi, 1)

                if ahead:
                    mit, mpar = after(it, par)
                    M = N + 1
                qk(0)
                qk(1)
                if ahead:
                    gelu(M)
                qk(2)
                qk(3)
                if ahead:
                    domain_hi(M, mpar)
                for u in range(4, 2 * KD):
                    qk(u)
                if ahead:
                    affine(M)

            act.wait_ge(prep, PREP)
            gelu(0)
            domain_hi(0, 0)
            affine(0, first=True)
            run(act, window)

        @block.vector
        def _(dve):
            steps = [0]

            def step(ins):
                steps[0] += 1
                ins.then_inc(prep, 1)
                dve.wait_ge(prep, steps[0])

            nc.vector.memset(onehot[:, :, :], 0.0).then_inc(main_free, RING)
            dve.wait_ge(small_loaded, 48)
            dve.wait_ge(main_free, RING)
            step(nc.vector.tensor_copy(idf[:, 0, :], idsi[:, :]))
            step(nc.vector.tensor_scalar(idf[:, 1, :], idf[:, 0, :], 0.0, float(EXPERTS - 1), ALU.max, ALU.min))
            step(nc.vector.tensor_tensor(idf[:, 2, :], idf[:, 0, :], idf[:, 1, :], ALU.is_equal))
            step(nc.vector.tensor_scalar(idf[:, 3, :], idf[:, 2, :], -1.0, 1.0, ALU.mult, ALU.add))
            for e in range(EXPERTS):
                ins = nc.vector.tensor_scalar(onehot[:, :, e], idf[:, 1, :], float(e), None, ALU.is_equal)
            step(ins)
            dve.wait_ge(stage_loaded[0], 32)
            nc.vector.tensor_copy(wdown[0][:, :, :], stage[0][:, :, 0:A]).then_inc(stage_hi, 1)
            wup4 = [w[:, :].rearrange("p (k n) -> p k n", k=KD) for w in wup]
            nc.vector.tensor_copy(wup4[0], stage[0][:, :, A:2 * A]).then_inc(stage_hi, 1)
            dve.wait_ge(stage_hi, 2)
            nc.vector.tensor_tensor(wdown[1][:, :, :], stage[0][:, :, 0:A], wdown[0][:, :, :].bitcast(F32), ALU.subtract)\
              .then_inc(stage_hi, 1)
            nc.vector.tensor_tensor(wup4[1], stage[0][:, :, A:2 * A], wup4[0].bitcast(F32), ALU.subtract)\
              .then_inc(stage_split, 1)

            def xsplit(M):
                dve.wait_ge(xt_loaded, 16 * M + 16)
                dve.wait_ge(down_done, M)
                nc.vector.tensor_copy(xts[0][:, :, :], xtf[:, :, :]).then_inc(xt_hi, 1)
                dve.wait_ge(xt_hi, M + 1)
                nc.vector.tensor_tensor(xts[1][:, :, :], xtf[:, :, :], xts[0][:, :, :].bitcast(F32), ALU.subtract)\
                  .then_inc(xt_split, 1)

            xsplit(0)
            dve.wait_ge(stage_loaded[1], 16)
            dve.wait_ge(ident_made, 3)
            experts = stage[1][:, :, :].rearrange("p k n -> p (k n)").rearrange("p (e o) -> p e o", e=EXPERTS)
            for b in range(BATCH):
                step(nc.vector.tensor_scalar(wexp_f[:, b, :], ident[:, :], idf[:, 3, b:b + 1], None, ALU.mult))
                step(nc.vector.tensor_scalar(esel[:, b, 0, :], onehot[:, b, :], idf[:, 2, b:b + 1], None, ALU.mult))
                for e in range(EXPERTS):
                    step(nc.vector.scalar_tensor_tensor(out=wexp_f[:, b, :], in0=experts[:, e, :],
                                                        scalar=esel[:, b, 0, e:e + 1], in1=wexp_f[:, b, :],
                                                        op0=ALU.mult, op1=ALU.add))
                step(nc.vector.tensor_tensor_reduce(esel[:, b, 1, :], col[:, C_EXPERT_B:C_EXPERT_B + EXPERTS],
                                                    esel[:, b, 0, :], 1.0, 0.0, ALU.mult, ALU.add, bexp[:, 0, b:b + 1]))
                step(nc.vector.tensor_tensor_reduce(esel[:, b, 1, :], col[:, C_EMB:C_EMB + EXPERTS],
                                                    onehot[:, b, :], 1.0, 0.0, ALU.mult, ALU.add, bexp[:, 1, b:b + 1]))
                step(nc.vector.tensor_tensor(bexp[:, 2, b:b + 1], bexp[:, 0, b:b + 1], bexp[:, 1, b:b + 1], ALU.add))
                step(nc.vector.tensor_copy(wexp[0][:, b, :], wexp_f[:, b, :]))
            assert steps[0] == PREP, steps[0]
            nc.vector.tensor_tensor(wexp[1][:, :, :], wexp_f[:, :, :], wexp[0][:, :, :].bitcast(F32), ALU.subtract)\
              .then_inc(stage_split, 1)

            def hidden_split(M):
                dve.wait_ge(gelu_done, M + 1)
                dve.wait_ge(expert_done, M)
                nc.vector.tensor_copy(hids[0][:, :], hid[:, :]).then_inc(hid_hi, 1)
                dve.wait_ge(hid_hi, M + 1)
                nc.vector.tensor_tensor(hids[1][:, :], hid[:, :], hids[0][:, :].bitcast(F32), ALU.subtract)\
                  .then_inc(hid_split, 1)

            def domain_lo(M, par):
                dve.wait_ge(dom_hi, M + 1)
                nc.vector.scalar_tensor_tensor(out=doms[1][:, :], in0=ps_mid[:, :], scalar=bexp[:, 2, par:par + 1],
                                               in1=doms[0][:, :].bitcast(F32), op0=ALU.add, op1=ALU.subtract)\
                  .then_inc(dom_split, 1)

            def residual(M, par):
                for t in range(TT):
                    dve.wait_ge(up_done, TT * M + t + 1)
                    dve.wait_ge(biased, TT * M + t + 1)
                    nc.vector.tensor_tensor(xn[par][:, t, :], ps_up[t % 2][:, :], xn[par][:, t, :], ALU.add)\
                      .then_inc(y_done, 1)

            def statistics(M, par, ln, ready):
                for t in range(TT):
                    dve.wait_ge(ready, TT * M + t + 1)
                    if t == 0:
                        dve.wait_ge(rstd_done, 2 * M + ln)
                    nc.vector.bn_stats(stats[:, ln, t, :], xn[par][:, t, :]).then_inc(stats_done, 1)

            def variance(M, ln):
                dve.wait_ge(stats_done, TT * (2 * M + ln) + TT)
                stand_alone(dve, passed)
                for t in range(TT):
                    nc.vector.bn_aggr(mean_var[:, ln, t, :], stats[:, ln, t, :]).then_inc(aggr_done, 1)
                dve.wait_ge(aggr_done, TT * (2 * M + ln) + TT)
                nc.vector.tensor_scalar(veps[:, ln, :], mean_var[:, ln, :, 1], EPS, None, ALU.add).then_inc(veps_done, 1)

            def first_norm(M, par):
                for t in range(TT):
                    nc.vector.scalar_tensor_tensor(out=xn[par][:, t, :], in0=xn[par][:, t, :],
                                                   scalar=mean_var[:, 0, t, 0:1], in1=row[:, R_LN_G, :],
                                                   op0=ALU.subtract, op1=ALU.mult).then_inc(scaled, 1)
                dve.wait_ge(rstd_done, 2 * M + 1)
                for t in range(TT):
                    dve.wait_ge(scaled, TT * M + t + 1)
                    nc.vector.scalar_tensor_tensor(out=xn[par][:, t, :], in0=xn[par][:, t, :],
                                                   scalar=rstd[:, 0, t:t + 1], in1=row[:, R_LN_B, :],
                                                   op0=ALU.mult, op1=ALU.add).then_inc(x0_done, 1)

            def second_norm(M, par):
                dve.wait_ge(rstd_done, 2 * M + 2)
                dve.wait_ge(tr_done, KD * M)
                for t in range(TT):
                    nc.vector.tensor_scalar(nrm[:, t, :], xn[par][:, t, :], mean_var[:, 1, t, 0:1],
                                            rstd[:, 1, t:t + 1], ALU.subtract, ALU.mult).then_inc(nrm_done, 1)

            def h_split(M, par, first=False):
                if not first:
                    dve.wait_ge(main_done, UNITS * (M - 1))
                for k in range(KD):
                    dve.wait_ge(htf_done, KD * M + k + 1)
                    nc.vector.tensor_copy(hts[par][0][:, k, :], htf[k % 2][:, :]).then_inc(ht_hi, 1)
                    dve.wait_ge(ht_hi, KD * M + k + 1)
                    nc.vector.tensor_tensor(hts[par][1][:, k, :], htf[k % 2][:, :],
                                            hts[par][0][:, k, :].bitcast(F32), ALU.subtract).then_inc(ht_split, 1)

            hidden_split(0)
            domain_lo(0, 0)
            residual(0, 0)
            statistics(0, 0, 0, y_done)
            variance(0, 0)
            for n in range(3):
                dve.wait_ge(stage_loaded[n % 2], 48 if n == 0 else (32 if n == 1 else 64))
                nc.vector.tensor_copy(wqkv[0][:, n, :, :], stage[n % 2][:, :, :]).then_inc(stage_hi, 1)
                dve.wait_ge(stage_hi, 4 + n)
                nc.vector.tensor_tensor(wqkv[1][:, n, :, :], stage[n % 2][:, :, :],
                                        wqkv[0][:, n, :, :].bitcast(F32), ALU.subtract).then_inc(stage_split, 1)
            first_norm(0, 0)
            statistics(0, 0, 1, x0_done)
            variance(0, 1)
            second_norm(0, 0)
            h_split(0, 0, first=True)

            def window(it, par, ahead, load):
                N = 2 * it + par
                M = N + 1
                mpar = 1 - par

                def qk(u):
                    dve.wait_ge(qk_hi, 2 * KD * N + u + 1)
                    nc.vector.scalar_tensor_tensor(out=qk_out[u % RING][:, 1, :], in0=ps_main[u % RING][:, :],
                                                   scalar=col[:, C_BQK + u:C_BQK + u + 1],
                                                   in1=qk_out[u % RING][:, 0, :].bitcast(F32),
                                                   op0=ALU.add, op1=ALU.subtract).then_inc(main_free, 1)

                def v(t):
                    dve.wait_ge(main_done, UNITS * N + 2 * KD + t + 1)
                    dve.wait_ge(v_stored[t % 2], 16 * (2 * N + t // 2))
                    nc.vector.tensor_tensor(v_out[t % 2][:, :], ps_main[t % RING][:, :], row[:, R_BV, :], ALU.add)\
                      .then_inc(main_free, 1)

                if ahead:
                    xsplit(M)
                qk(0)
                qk(1)
                if ahead:
                    hidden_split(M)
                qk(2)
                qk(3)
                if ahead:
                    domain_lo(M, mpar)
                qk(4)
                qk(5)
                if ahead:
                    residual(M, mpar)
                    statistics(M, mpar, 0, y_done)
                qk(6)
                if ahead:
                    variance(M, 0)
                qk(7)
                if ahead:
                    first_norm(M, mpar)
                v(0)
                if ahead:
                    statistics(M, mpar, 1, x0_done)
                    variance(M, 1)
                v(1)
                if ahead:
                    second_norm(M, mpar)
                v(2)
                if ahead:
                    h_split(M, mpar)
                v(3)

            run(dve, window)

        @block.tensor
        def _(pe):
            def down(M):
                pe.wait_ge(xt_split, M + 1)
                pe.wait_ge(dom_split, M)
                for k in range(KD):
                    last = product3(pe, ps_mid[:, :], [w[:, k, :] for w in wdown], [v[:, k, :] for v in xts],
                                    k == 0, k == KD - 1)
                last.then_inc(down_done, 1)

            def expert(M, par):
                pe.wait_ge(hid_split, M + 1)
                product3(pe, ps_mid[:, :], [w[:, par, :] for w in wexp], [v[:, :] for v in hids], True, True)\
                  .then_inc(expert_done, 1)

            def up(M):
                pe.wait_ge(dom_split, M + 1)
                for t in range(TT):
                    if t >= 2:
                        pe.wait_ge(y_done, TT * M + t - 1)
                    product3(pe, ps_up[t % 2][:, :], [v[:, t * P:(t + 1) * P] for v in doms],
                             [w[:, :] for w in wup], True, True).then_inc(up_done, 1)

            def transposes(M):
                pe.wait_ge(nrm_done, TT * M + TT)
                for k in range(KD):
                    pe.wait_ge(htf_done, KD * M + k)
                    for t in range(TT):
                        last = pe.transpose(ps_tr[:, t * P:(t + 1) * P], nrm[:, t, k * P:(k + 1) * P], ident[:, :])
                    last.then_inc(tr_done, 1)

            def window(it, par, ahead, load):
                N = 2 * it + par
                M = N + 1

                def qk(u):
                    pe.wait_ge(main_free, UNITS * N + u + 1)
                    if u % KD < 1:
                        pe.wait_ge(ht_split, KD * N + KD)
                    w = [z[:, u // KD, :, (u % KD) * P:(u % KD + 1) * P] for z in wqkv]
                    for k in range(KD):
                        last = product3(pe, ps_main[u % RING][:, :], [z[:, k, :] for z in w],
                                        [z[:, k, :] for z in hts[par]], k == 0, k == KD - 1)
                    last.then_inc(main_done, 1)

                def v(t):
                    pe.wait_ge(main_free, UNITS * N + 2 * KD + t + 1)
                    for k in range(KD):
                        last = product3(pe, ps_main[t % RING][:, :], [z[:, k, t * P:(t + 1) * P] for z in hts[par]],
                                        [z[:, 2, k, :] for z in wqkv], k == 0, k == KD - 1)
                    last.then_inc(main_done, 1)

                qk(0)
                qk(1)
                if ahead:
                    down(M)
                qk(2)
                qk(3)
                if ahead:
                    expert(M, 1 - par)
                qk(4)
                qk(5)
                if ahead:
                    up(M)
                qk(6)
                qk(7)
                v(0)
                v(1)
                v(2)
                if ahead:
                    transposes(M)
                v(3)

            pe.wait_ge(stage_split, 1)
            down(0)
            pe.wait_ge(stage_split, 2)
            expert(0, 0)
            up(0)
            pe.wait_ge(ident_made, 3)
            transposes(0)
            pe.wait_ge(stage_split, 5)
            run(pe, window)


def attend(nc, qk_s, v_s, ctx_s):
    QB = 512
    HG = 4
    NQ = SEQ // QB
    KT = SEQ // P
    PAIRS = HEADS // HG
    ROWS, MROWS = 3 * DH, 3 * DH + 2
    SCALE = float(1.0 / DH ** 0.5)
    AHEAD = 90
    QT = QB // P

    def scores(j):
        return [("s", j, h, q, c) for q in range(QT) for c in range(j + 1) for h in range(HG)]

    stream = scores(0)
    for j in range(1, NQ):
        more = scores(j)
        stream += more[:4] + [("t", j - 1)] + more[4:]
    own = [(0, u) for u in stream[AHEAD:]]
    nxt = [(1, u) for u in stream[:AHEAD]]
    units = own + nxt[:4] + [(0, ("t", NQ - 1))] + nxt[4:]
    UNITS = len(units)

    steps = [(j, k) for j in range(NQ) for k in range(QT * (j + 1))]
    STEPS = len(steps)

    def offset(j, k):
        return max(0, k - QT * j) * P

    def shares(last):
        work = [QB - offset(*s) + 64 for s in steps]
        total, done, out, at = sum(work), 0, [], 0
        for w in work:
            done += w
            upto = len(units) * done // total
            out.append([u for u in units[at:upto] if not (last and u[0])])
            at = upto
        return out

    ctx = ExitStack()
    with ctx:
        def sb(name, shape, dt=F32):
            return ctx.enter_context(nc.sbuf_tensor(name, shape, dt))

        def sem(name):
            return ctx.enter_context(nc.semaphore(name))

        qs = [sb(f"q_stack{i}", [P, NQ, HG, QB], F32R) for i in range(2)]
        ks = [sb(f"k_stack{i}", [P, HG, SEQ], F32R) for i in range(2)]
        vt = [sb(f"v_tiles{i}", [P, KT, HG * DH]) for i in range(2)]
        probs = [sb(f"probs{i}", [P, HG, QB]) for i in range(2)]
        ident = sb("ident_b", [P, P])
        ones = sb("ones_b", [P, DH])
        mask = sb("mask_b", [P, QB])
        causal_f = sb("causal_f", [P, P])
        causal = sb("causal", [P, P], BF16)
        ident_h = sb("ident_h", [P, P], BF16)
        junk = sb("junk_b", [P, 2, QB])
        mpart = sb("mpart", [P, 2, HG * QT, NQ])
        mrow = sb("mrow", [P, 2, 2, HG * QT])
        mhi = sb("mhi", [P, 2, HG * QT], F32R)
        mcol = sb("mcol", [P, 2, 2, HG * QT])
        mturn = sb("mturn", [2 * HG * QT, 2, P])
        o_sb = sb("o_sb", [P, QB])
        sum_t = sb("sum_t", [P, QB // DH, DH])
        rec = sb("rec", [P, QB // DH])
        rec_t = sb("rec_t", [P, QB // DH, DH])
        rec_b = sb("rec_b", [P, QB])
        cx = sb("cx", [P, 2, QB])
        ps_m = [ctx.enter_context(nc.psum_tensor(f"ps_m{i}", [P, QB], F32)) for i in range(2)]
        ps_s = [ctx.enter_context(nc.psum_tensor(f"ps_s{i}", [P, 2, QB], F32)) for i in range(2)]
        ps_o = ctx.enter_context(nc.psum_tensor("ps_o", [P, QB], F32))
        ps_sum = ctx.enter_context(nc.psum_tensor("ps_sum", [P, QB], F32))

        consts = sem("consts_b")
        half_consts = sem("half_consts")
        passed = sem("passed_b")
        loaded = [sem(f"stacks_loaded{i}") for i in range(2)]
        unit_done = sem("unit_done")
        unit_free = sem("unit_free")
        max_done = sem("max_done")
        neg_done = sem("neg_done")
        mhi_done = sem("mhi_done")
        mcol_done = sem("mcol_done")
        m_stacked = [sem(f"m_stacked{i}") for i in range(2)]
        s_done = sem("s_done")
        exp_done = [sem(f"exp_done{i}") for i in range(2)]
        pv_done = sem("pv_done")
        sum_turned = sem("sum_turned")
        o_free = sem("o_free")
        rec_done = sem("rec_done")
        rec_spread = sem("rec_spread")
        rec_turned = sem("rec_turned")
        ctx_done = sem("ctx_done")
        ctx_stored = [sem(f"ctx_stored{i}") for i in range(2)]

        def run(eng, window):
            with eng.Fori(0, PAIRS - 1) as it:
                window(it, 0, False)
                window(it, 1, False)
            window(PAIRS - 1, 0, False)
            window(PAIRS - 1, 1, True)

        def behind(it, par):
            return (it, 1) if par == 0 else (it + 1, 0)

        block = ctx.enter_context(nc.Block())

        @block.sync
        def _(sp):
            def load(it, par):
                samples = slice(par * SEQ, (par + 1) * SEQ)
                for r, part in enumerate((0, 1, 0)):
                    sp.dma_start(ks[par][r * DH:(r + 1) * DH, :, :].bitcast(F32),
                                 qk_s[1, bass.ds(it * P, P), part, samples].rearrange("(h p) t -> p h t", p=DH))\
                      .then_inc(loaded[par], 16)
                for j in range(NQ):
                    for r, part in enumerate((0, 0, 1)):
                        sp.dma_start(qs[par][r * DH:(r + 1) * DH, j, :, :].bitcast(F32),
                                     qk_s[0, bass.ds(it * P, P), part, par * SEQ + j * QB:par * SEQ + (j + 1) * QB]
                                     .rearrange("(h p) t -> p h t", p=DH)).then_inc(loaded[par], 16)
                sp.dma_start(vt[par][:, :, :],
                             v_s[samples, bass.ds(it * P, P)].rearrange("(t p) d -> p t d", p=P)).then_inc(loaded[par], 16)

            def stack_max(it, par, j, index):
                sp.wait_ge(unit_free, 2 + index + 1)
                for part in range(2):
                    sp.dma_start(qs[par][ROWS + part:ROWS + part + 1, j, :, :].rearrange("p h t -> p (h t)").bitcast(F32),
                                 mturn[part * HG * QT:(part + 1) * HG * QT, j % 2, :])\
                      .then_inc(m_stacked[j % 2], 16)

            def store(it, par, j):
                sp.wait_ge(ctx_done, NQ * (2 * it + par) + j + 1)
                stand_alone(sp, passed)
                sp.dma_start(ctx_s[bass.ds(it * P, P), par * SEQ + j * QB:par * SEQ + (j + 1) * QB],
                             cx[:, j % 2, :]).then_inc(ctx_stored[j % 2], 16)

            def window(it, par, last):
                W = 2 * it + par
                if not last:
                    sp.wait_ge(pv_done, STEPS * W)
                    stand_alone(sp, passed)
                    load(*behind(it, par))
                i = AHEAD
                for n, share in enumerate(shares(last)):
                    for ahead, u in share:
                        if u[0] == "t":
                            stack_max(*(behind(it, par) if ahead else (it, par)), u[1], UNITS * W + i)
                        i += 1
                    if n and steps[n][1] == 0:
                        store(it, par, steps[n][0] - 1)
                store(it, par, NQ - 1)

            load(0, 0)
            for i, u in enumerate(stream[:AHEAD]):
                if u[0] == "t":
                    stack_max(0, 0, u[1], i)
            run(sp, window)
            for i in range(2):
                sp.wait_ge(ctx_stored[i], 16 * 2 * PAIRS * NQ // 2)

        @block.gpsimd
        def _(pool):
            make_identity(pool, ident[:, :], consts)
            pool.memset(ones[:, :], 1.0).then_inc(consts, 1)
            for i in range(2):
                pool.wait_ge(consts, 3 + i)
                pool.memset(ks[i][ROWS:MROWS, :, :].bitcast(F32), 1.0).then_inc(consts, 1)
            pool.wait_ge(consts, 5)
            pool.memset(mask[:, :], 0.0).then_inc(consts, 1)
            pool.wait_ge(consts, 6)
            pool.affine_select(out=causal_f[:, :], in_=mask[:, 0:P], compare_op=ALU.is_ge, fill=-1.0e30, base=0,
                               pattern=[[1, P]], channel_multiplier=-1).then_inc(consts, 1)
            pool.affine_select(out=mask[:, QB - P:], in_=mask[:, QB - P:], compare_op=ALU.is_ge, fill=LOWEST, base=0,
                               pattern=[[-1, P]], channel_multiplier=1).then_inc(consts, 1)

        @block.scalar
        def _(act):
            def window(it, par, last):
                G = STEPS * (2 * it + par)
                for n, (j, k) in enumerate(steps):
                    off = offset(j, k)
                    for pair in range(2):
                        act.wait_ge(s_done, 2 * (G + n) + pair + 1)
                        nc.scalar.activation(probs[n % 2][:, 2 * pair:2 * pair + 2, off:], ps_s[pair][:, :, off:],
                                             ACT.Exp, scale=SCALE).then_inc(exp_done[pair], 1)

            run(act, window)

        @block.vector
        def _(dve):
            nc.vector.memset(junk[:, :, :], 0.0).then_inc(unit_free, 2)
            dve.wait_ge(consts, 8)
            nc.vector.tensor_copy(causal[:, :], causal_f[:, :]).then_inc(half_consts, 1)
            nc.vector.tensor_copy(ident_h[:, :], ident[:, :]).then_inc(half_consts, 1)

            def unit(it, par, u, index, slot):
                W = 2 * it + par
                dve.wait_ge(unit_done, index + 1)
                if u[0] == "t":
                    j = u[1]
                    before = 32 * (2 * W + j // 2)
                    dve.wait_ge(m_stacked[j % 2], before)
                    nc.vector.tensor_copy(mturn[:, j % 2, :], ps_m[slot][0:2 * HG * QT, 0:P]).then_inc(unit_free, 1)
                    return
                _, j, h, q, c = u
                out = mpart[:, j % 2, h * QT + q, c:c + 1]
                if c < j:
                    nc.vector.tensor_reduce(out, ps_m[slot][:, :], AX.X, ALU.max).then_inc(unit_free, 1)
                else:
                    stand_alone(dve, passed)
                    w = (q + 1) * P
                    nc.vector.tensor_tensor_reduce(junk[:, slot, 0:w], ps_m[slot][:, 0:w], mask[:, QB - w:], 1.0, LOWEST,
                                                   ALU.add, ALU.max, out).then_inc(unit_free, 1)

            def finish_max(it, par, j, index):
                B = NQ * (2 * it + par) + j
                b = j % 2
                dve.wait_ge(unit_free, 2 + index + 1)
                nc.vector.tensor_reduce(mrow[:, b, 0, :], mpart[:, b, :, 0:j + 1], AX.X, ALU.max).then_inc(max_done, 1)
                dve.wait_ge(max_done, B + 1)
                nc.vector.tensor_scalar(mrow[:, b, 1, :], mrow[:, b, 0, :], -1.0, None, ALU.mult).then_inc(neg_done, 1)
                dve.wait_ge(neg_done, B + 1)
                nc.vector.tensor_copy(mhi[:, b, :], mrow[:, b, 1, :]).then_inc(mhi_done, 1)
                dve.wait_ge(mhi_done, B + 1)
                nc.vector.tensor_copy(mcol[:, b, 0, :], mhi[:, b, :].bitcast(F32)).then_inc(mcol_done, 1)
                nc.vector.tensor_tensor(mcol[:, b, 1, :], mrow[:, b, 1, :], mhi[:, b, :].bitcast(F32), ALU.subtract)\
                  .then_inc(mcol_done, 1)

            def normalise(it, par, j):
                B = NQ * (2 * it + par) + j
                done = sum(1 for s in steps if s[0] <= j)
                dve.wait_ge(pv_done, STEPS * (2 * it + par) + done)
                nc.vector.transpose(sum_t[:, :, :].rearrange("p c i -> p (c i)"), ps_sum[:, :]).then_inc(sum_turned, 1)
                dve.wait_ge(ctx_done, B)
                nc.vector.tensor_copy(o_sb[:, :], ps_o[:, :]).then_inc(o_free, 1)
                dve.wait_ge(sum_turned, B + 1)
                nc.vector.reciprocal(rec[:, :], sum_t[:, :, 0]).then_inc(rec_done, 1)
                dve.wait_ge(rec_done, B + 1)
                nc.vector.tensor_copy(rec_t[:, :, :], rec[:, :].unsqueeze(2).to_broadcast([P, QB // DH, DH]))\
                  .then_inc(rec_spread, 1)
                dve.wait_ge(rec_spread, B + 1)
                nc.vector.transpose(rec_b[:, :], rec_t[:, :, :].rearrange("p c i -> p (c i)")).then_inc(rec_turned, 1)
                dve.wait_ge(rec_turned, B + 1)
                dve.wait_ge(o_free, B + 1)
                dve.wait_ge(ctx_stored[j % 2], 16 * (2 * (2 * it + par) + j // 2))
                nc.vector.tensor_tensor(cx[:, j % 2, :], o_sb[:, :], rec_b[:, :], ALU.mult).then_inc(ctx_done, 1)

            def last_of(u):
                return u[0] == "s" and u == scores(u[1])[-1]

            def do(it, par, u, base, i):
                unit(it, par, u, base + i, i % 2)
                if last_of(u):
                    finish_max(it, par, u[1], base + i)

            for i, u in enumerate(stream[:AHEAD]):
                do(0, 0, u, 0, i)

            def window(it, par, last):
                base = UNITS * (2 * it + par)
                i = AHEAD
                for n, share in enumerate(shares(last)):
                    for ahead, u in share:
                        do(*(behind(it, par) if ahead else (it, par)), u, base, i)
                        i += 1
                    if n and steps[n][1] == 0:
                        normalise(it, par, steps[n][0] - 1)
                normalise(it, par, NQ - 1)

            run(dve, window)

        @block.tensor
        def _(pe):
            pe.wait_ge(consts, 8)
            pe.wait_ge(half_consts, 2)

            def unit(it, par, u, base, i):
                pe.wait_ge(unit_free, base + i + 1)
                if u[0] == "t":
                    j = u[1]
                    pe.wait_ge(mcol_done, 2 * (NQ * (2 * it + par) + j) + 2)
                    pe.transpose(ps_m[i % 2][0:2 * HG * QT, 0:P], mcol[:, j % 2, :, :].rearrange("p a n -> p (a n)"),
                                 ident[:, :]).then_inc(unit_done, 1)
                    return
                _, j, h, q, c = u
                if u == stream[0]:
                    pe.wait_ge(loaded[par], 16 * (4 + 3 * NQ) * (it + 1))
                w = QB if c < j else (q + 1) * P
                pe.matmul(ps_m[i % 2][:, 0:w], qs[par][0:ROWS, j, h, q * P:(q + 1) * P], ks[par][0:ROWS, h, c * QB:c * QB + w],
                          start=True, stop=True).then_inc(unit_done, 1)

            for i, u in enumerate(stream[:AHEAD]):
                unit(0, 0, u, 0, i)

            def window(it, par, last):
                W = 2 * it + par
                G = STEPS * W
                at = [AHEAD]

                def some(share):
                    for ahead, u in share:
                        unit(*(behind(it, par) if ahead else (it, par)), u, UNITS * W, at[0])
                        at[0] += 1

                def probabilities(n, pair):
                    j, k = steps[n]
                    off = offset(j, k)
                    if k == 0 and pair == 0:
                        pe.wait_ge(m_stacked[j % 2], 32 * (2 * W + j // 2 + 1))
                    pe.wait_ge(exp_done[pair], G + n)
                    for h in (2 * pair, 2 * pair + 1):
                        mm = pe.matmul(ps_s[pair][:, h % 2, off:], ks[par][0:MROWS, h, k * P:(k + 1) * P],
                                       qs[par][0:MROWS, j, h, off:], start=True, stop=k < QT * j)
                        if k >= QT * j:
                            mm = pe.matmul(ps_s[pair][:, h % 2, off:off + P], ident_h[:, :], causal[:, :],
                                           start=False, stop=True)
                    mm.then_inc(s_done, 1)

                def weigh(n):
                    j, k = steps[n]
                    off = offset(j, k)
                    for pair in range(2):
                        pe.wait_ge(exp_done[pair], G + n + 1)
                    if k == 0:
                        pe.wait_ge(o_free, NQ * W + j)
                    for h in range(HG):
                        pe.matmul(ps_o[h * DH:(h + 1) * DH, off:], vt[par][:, k, h * DH:(h + 1) * DH],
                                  probs[n % 2][:, h, off:], start=(k == 0), stop=(k == QT * (j + 1) - 1))

                def add_up(n):
                    j, k = steps[n]
                    off = offset(j, k)
                    for h in range(HG):
                        mm = pe.matmul(ps_sum[h * DH:(h + 1) * DH, off:], ones[:, :], probs[n % 2][:, h, off:],
                                       start=(k == 0), stop=(k == QT * (j + 1) - 1))
                    mm.then_inc(pv_done, 1)

                for n, share in enumerate(shares(last)):
                    q = (len(share) + 3) // 4
                    probabilities(n, 0)
                    some(share[:q])
                    probabilities(n, 1)
                    some(share[q:2 * q])
                    if n:
                        weigh(n - 1)
                    some(share[2 * q:3 * q])
                    if n:
                        add_up(n - 1)
                    some(share[3 * q:])
                weigh(STEPS - 1)
                add_up(STEPS - 1)

            run(pe, window)


def mlp(nc, ctx_s, x0_s, cols, rows, gates, wo, w1, w2, out):
    T = 256
    TT = T // P
    PAIRS = SEQ // T
    HALF = 2 * D
    PROJECT_AT, TURN_AT = 3, 12

    ctx = ExitStack()
    with ctx:
        def sb(name, shape, dt=F32):
            return ctx.enter_context(nc.sbuf_tensor(name, shape, dt))

        def sem(name):
            return ctx.enter_context(nc.semaphore(name))

        w1s = [sb("w1_hi", [P, KD, F], F32R), sb("w1_lo", [P, KD, F], F32R)]
        w2s = [sb("w2_hi", [P, KF, D], F32R), sb("w2_lo", [P, KF, D], F32R)]
        wos = [sb("wo_hi", [P, KD, D], F32R), sb("wo_lo", [P, KD, D], F32R)]
        col = sb("col_c", [P, COLS])
        bo = sb("bo_row", [P, D])
        gb2 = sb("gb2", [P, BATCH, D])
        gate = sb("gate", [P, 2, BATCH])
        ident = sb("ident_c", [P, P])
        half = sb("half_c", [P, TT])
        xg = [sb(f"xg{i}", [P, TT, D]) for i in range(2)]
        x1 = sb("x1", [P, TT, D])
        cf = sb("cf", [P, KD, T])
        cts = [sb("ct_hi", [P, KD, T], F32R), sb("ct_lo", [P, KD, T], F32R)]
        htf = [sb(f"h2f{i}", [P, T]) for i in range(2)]
        hts = [[sb(f"h2_hi{i}", [P, KD, T], F32R), sb(f"h2_lo{i}", [P, KD, T], F32R)] for i in range(2)]
        act_f = [sb(f"act_f{i}", [P, T]) for i in range(2)]
        acts = [[sb(f"act_hi{i}", [P, T], F32R), sb(f"act_lo{i}", [P, T], F32R)] for i in range(2)]
        stats = sb("stats_c", [P, TT, 6])
        mean_var = sb("mean_var_c", [P, TT, 2])
        veps = sb("veps_c", [P, TT])
        rstd = sb("rstd_c", [P, TT])
        ps_acc = [ctx.enter_context(nc.psum_tensor(f"ps_acc{i}", [P, D], F32)) for i in range(TT)]
        ps_h = [ctx.enter_context(nc.psum_tensor(f"ps_h{i}", [P, 512], F32)) for i in range(2)]
        ps_p = [ctx.enter_context(nc.psum_tensor(f"ps_p{i}", [P, D], F32)) for i in range(TT)]
        ps_tr = [ctx.enter_context(nc.psum_tensor(f"ps_tr_c{i}", [P, 512], F32)) for i in range(2)]

        small_loaded = sem("small_loaded_c")
        ident_made = sem("ident_made_c")
        passed = sem("passed_c")
        w_loaded = [sem(f"w_loaded{i}") for i in range(2)]
        w_hi = sem("w_hi")
        w_split = sem("w_split")
        prep = sem("prep_c")
        xg_loaded = [sem(f"xg_loaded{i}") for i in range(2)]
        ctx_loaded = sem("ctx_loaded")
        ctx_hi = sem("ctx_hi")
        ctx_split = sem("ctx_split")
        with_bo = sem("with_bo")
        kept = sem("kept")
        kept_b = sem("kept_b")
        projected = sem("projected")
        x1_done = sem("x1_done")
        stats_done = sem("stats_done_c")
        aggr_done = sem("aggr_done_c")
        veps_done = sem("veps_done_c")
        rstd_done = sem("rstd_done_c")
        z_done = sem("z_done")
        nrm_done = sem("nrm_done_c")
        tr_done = sem("tr_done_c")
        htf_done = sem("htf_done_c")
        ht_hi = sem("ht_hi_done_c")
        ht_split = sem("ht_split_c")
        h_done = sem("h_done")
        gelu_done = sem("gelu_done_c")
        act_hi = sem("act_hi")
        act_split = sem("act_split")
        y_done = sem("y_done_c")
        acc_free = sem("acc_free")
        out_stored = [sem(f"out_stored{i}") for i in range(2)]

        pieces = [(wos, wo, n) for n in range(2)]
        pieces += [(w1s, w1, n) for n in range(2 * KD)]
        pieces += [(w2s, w2, n) for n in range(KF // 2)]

        def piece_of(dst, n):
            flat = dst[:, :, :].rearrange("p k n -> p (k n)")
            return flat[:, n * HALF:(n + 1) * HALF]

        def piece_in(w, n):
            width = w.shape[1]
            if width == F:
                return w[(n // 2) * P:(n // 2 + 1) * P, (n % 2) * HALF:(n % 2 + 1) * HALF]
            return w[2 * n * P:2 * (n + 1) * P, :].rearrange("(k p) n -> p k n", p=P)

        stage = [xg[1], x1]

        def run(eng, window):
            with eng.Fori(0, PAIRS - 1) as it:
                window(it, 0, True, True)
                window(it, 1, True, True)
            window(PAIRS - 1, 0, True, False)
            window(PAIRS - 1, 1, False, False)

        def tokens(it, par):
            return bass.ds(it * T + par * SEQ, T)

        block = ctx.enter_context(nc.Block())

        @block.sync
        def _(sp):
            def load_ctx(it, par):
                sp.dma_start(cf[:, :, :], ctx_s.rearrange("(k p) t -> p k t", p=P)[:, :, tokens(it, par)])\
                  .then_inc(ctx_loaded, 16)

            def load_x(it, par):
                sp.dma_start(xg[par][:, :, :], x0_s[tokens(it, par), :].rearrange("(t p) d -> p t d", p=P))\
                  .then_inc(xg_loaded[par], 16)

            load_ctx(0, 0)
            load_x(0, 0)
            sp.dma_start(col[:, :], cols).then_inc(small_loaded, 16)
            sp.dma_start(gate[:, 0, :], gates).then_inc(small_loaded, 16)
            sp.dma_start(bo[:, :], rows[:, R_BO, :]).then_inc(small_loaded, 16)
            for b in range(BATCH):
                sp.dma_start(gb2[:, b, :], rows[:, R_B2, :]).then_inc(small_loaded, 16)
            for n, (_, w, i) in enumerate(pieces):
                if n >= 2:
                    sp.wait_ge(w_split, n - 1)
                src = piece_in(w, i)
                dst = stage[n % 2][:, :, :]
                if len(src.shape) == 2:
                    dst = dst.rearrange("p t n -> p (t n)")
                sp.dma_start(dst, src).then_inc(w_loaded[n % 2], 16)
            sp.wait_ge(ctx_split, 1)
            load_ctx(0, 1)
            sp.wait_ge(w_split, len(pieces))
            load_x(0, 1)

            def window(it, par, ahead, load):
                N = 2 * it + par
                if load:
                    sp.wait_ge(ctx_split, N + 2)
                    stand_alone(sp, passed)
                    load_ctx(it + 1, par)
                sp.wait_ge(acc_free, TT * N + TT)
                stand_alone(sp, passed)
                sp.dma_start(out[tokens(it, par), :].rearrange("(t p) d -> p t d", p=P), xg[par][:, :, :])\
                  .then_inc(out_stored[par], 16)
                if load:
                    sp.wait_ge(out_stored[par], 16 * it + 16)
                    load_x(it + 1, par)

            run(sp, window)
            for par in range(2):
                sp.wait_ge(out_stored[par], 16 * PAIRS)

        @block.gpsimd
        def _(pool):
            make_identity(pool, ident[:, :], ident_made)
            pool.memset(half[:, :], -0.5).then_inc(ident_made, 1)
            pool.wait_ge(ident_made, 3)
            pool.wait_ge(small_loaded, 80)
            pool.wait_ge(prep, 3)

            def chunk(it, par, M):
                pool.wait_ge(xg_loaded[par], 16 * it + 16)
                pool.wait_ge(tr_done, KD * M)
                for t in range(TT):
                    pool.tensor_tensor(x1[:, t, :], xg[par][:, t, :], bo[:, :], ALU.add).then_inc(with_bo, 1)
                pool.wait_ge(with_bo, TT * M + TT)
                stand_alone(pool, passed)
                for t in range(TT):
                    pool.tensor_scalar(xg[par][:, t, :], xg[par][:, t, :], gate[:, 1, par:par + 1], None, ALU.mult)\
                        .then_inc(kept, 1)
                for t in range(TT):
                    pool.wait_ge(kept, TT * M + t + 1)
                    pool.tensor_tensor(xg[par][:, t, :], xg[par][:, t, :], gb2[:, par, :], ALU.add).then_inc(kept_b, 1)
                pool.wait_ge(veps_done, M + 1)
                pool.tensor_tensor(rstd[:, :], veps[:, :], half[:, :], ALU.pow).then_inc(rstd_done, 1)

            def window(it, par, ahead, load):
                if ahead:
                    mit, mpar = (it, 1) if par == 0 else (it + 1, 0)
                    chunk(mit, mpar, 2 * it + par + 1)

            pool.wait_ge(w_split, len(pieces))
            chunk(0, 0, 0)
            run(pool, window)

        @block.scalar
        def _(act):
            act.wait_ge(small_loaded, 80)
            for n, (dst, _, i) in enumerate(pieces):
                act.wait_ge(w_loaded[n % 2], 16 * (n // 2 + 1))
                nc.scalar.activation(piece_of(dst[0], i), stage[n % 2][:, :, :].rearrange("p t n -> p (t n)"), ACT.Copy)\
                  .then_inc(w_hi, 1)

            def affine(M, k, first=False):
                act.wait_ge(tr_done, KD * M + k + 1)
                if k >= 2 or not first:
                    act.wait_ge(ht_split, KD * M + k - 1)
                nc.scalar.activation(htf[k % 2][:, :], ps_tr[k % 2][:, 0:T], ACT.Identity,
                                     scale=col[:, C_G2 + k:C_G2 + k + 1],
                                     bias=col[:, C_B2LN + k:C_B2LN + k + 1]).then_inc(htf_done, 1)

            def window(it, par, ahead, load):
                N = 2 * it + par
                for f in range(KF):
                    act.wait_ge(h_done, KF * N + f + 1)
                    act.wait_ge(act_split, 2 + KF * N + f - 1)
                    nc.scalar.activation(act_f[f % 2][:, :], ps_h[f % 2][:, 0:T], ACT.Gelu,
                                         bias=col[:, C_MLP_B1 + f:C_MLP_B1 + f + 1]).then_inc(gelu_done, 1)
                    if ahead and f == TURN_AT:
                        for k in range(KD):
                            affine(N + 1, k)

            for k in range(KD):
                affine(0, k, first=True)
            run(act, window)

        @block.vector
        def _(dve):
            dve.wait_ge(small_loaded, 80)
            nc.vector.tensor_scalar(gate[:, 1, :], gate[:, 0, :], -1.0, 1.0, ALU.mult, ALU.add).then_inc(prep, 1)
            for b in range(BATCH):
                nc.vector.tensor_scalar(gb2[:, b, :], gb2[:, b, :], gate[:, 0, b:b + 1], None, ALU.mult).then_inc(prep, 1)
            nc.vector.memset(stats[:, :, :], 0.0).then_inc(act_split, 2)
            nc.vector.memset(mean_var[:, :, :], 0.0).then_inc(y_done, 2)
            dve.wait_ge(act_split, 2)
            dve.wait_ge(y_done, 2)

            def ctx_halves(M):
                dve.wait_ge(ctx_loaded, 16 * M + 16)
                dve.wait_ge(projected, TT * M)
                nc.vector.tensor_copy(cts[0][:, :, :], cf[:, :, :]).then_inc(ctx_hi, 1)
                dve.wait_ge(ctx_hi, M + 1)
                nc.vector.tensor_tensor(cts[1][:, :, :], cf[:, :, :], cts[0][:, :, :].bitcast(F32), ALU.subtract)\
                  .then_inc(ctx_split, 1)

            ctx_halves(0)
            for n, (dst, _, i) in enumerate(pieces):
                dve.wait_ge(w_hi, n + 1)
                nc.vector.tensor_tensor(piece_of(dst[1], i), stage[n % 2][:, :, :].rearrange("p t n -> p (t n)"),
                                        piece_of(dst[0], i).bitcast(F32), ALU.subtract).then_inc(w_split, 1)

            def residual(M, t):
                dve.wait_ge(projected, TT * M + t + 1)
                dve.wait_ge(with_bo, TT * M + TT)
                nc.vector.tensor_tensor(x1[:, t, :], ps_p[t][:, :], x1[:, t, :], ALU.add).then_inc(x1_done, 1)

            def statistics(M, t):
                dve.wait_ge(x1_done, TT * M + t + 1)
                nc.vector.bn_stats(stats[:, t, :], x1[:, t, :]).then_inc(stats_done, 1)

            def variance(M):
                dve.wait_ge(stats_done, TT * M + TT)
                stand_alone(dve, passed)
                for t in range(TT):
                    nc.vector.bn_aggr(mean_var[:, t, :], stats[:, t, :]).then_inc(aggr_done, 1)
                dve.wait_ge(aggr_done, TT * M + TT)
                nc.vector.tensor_scalar(veps[:, :], mean_var[:, :, 1], EPS, None, ALU.add).then_inc(veps_done, 1)

            def keep(M, par, t):
                dve.wait_ge(kept_b, TT * M + t + 1)
                nc.vector.scalar_tensor_tensor(out=xg[par][:, t, :], in0=x1[:, t, :], scalar=gate[:, 0, par:par + 1],
                                               in1=xg[par][:, t, :], op0=ALU.mult, op1=ALU.add).then_inc(z_done, 1)

            def normalise(M, t):
                dve.wait_ge(rstd_done, M + 1)
                dve.wait_ge(z_done, TT * M + t + 1)
                nc.vector.tensor_scalar(x1[:, t, :], x1[:, t, :], mean_var[:, t, 0:1], rstd[:, t:t + 1],
                                        ALU.subtract, ALU.mult).then_inc(nrm_done, 1)

            def h_split(M, par, k):
                dve.wait_ge(htf_done, KD * M + k + 1)
                nc.vector.tensor_copy(hts[par][0][:, k, :], htf[k % 2][:, :]).then_inc(ht_hi, 1)
                dve.wait_ge(ht_hi, KD * M + k + 1)
                nc.vector.tensor_tensor(hts[par][1][:, k, :], htf[k % 2][:, :],
                                        hts[par][0][:, k, :].bitcast(F32), ALU.subtract).then_inc(ht_split, 1)

            for t in range(TT):
                residual(0, t)
                statistics(0, t)
            variance(0)
            for t in range(TT):
                keep(0, 0, t)
            for t in range(TT):
                normalise(0, t)
            for k in range(KD):
                h_split(0, 0, k)

            def window(it, par, ahead, load):
                N = 2 * it + par
                M = N + 1
                mpar = 1 - par

                def gelu_split(f):
                    dve.wait_ge(gelu_done, KF * N + f + 1)
                    dve.wait_ge(y_done, KF * N + f + 1)
                    nc.vector.tensor_copy(acts[f % 2][0][:, :], act_f[f % 2][:, :]).then_inc(act_hi, 1)
                    dve.wait_ge(act_hi, KF * N + f + 1)
                    nc.vector.tensor_tensor(acts[f % 2][1][:, :], act_f[f % 2][:, :],
                                            acts[f % 2][0][:, :].bitcast(F32), ALU.subtract).then_inc(act_split, 1)

                for f in range(KF):
                    gelu_split(f)
                    if ahead:
                        if f == 1:
                            ctx_halves(M)
                        if PROJECT_AT < f <= PROJECT_AT + TT:
                            residual(M, f - PROJECT_AT - 1)
                            statistics(M, f - PROJECT_AT - 1)
                        if f == PROJECT_AT + TT + 1:
                            variance(M)
                        if f == PROJECT_AT + TT + 2:
                            for t in range(TT):
                                keep(M, mpar, t)
                        if f == PROJECT_AT + TT + 3:
                            for t in range(TT):
                                normalise(M, t)
                        if f == TURN_AT:
                            for k in range(KD):
                                h_split(M, mpar, k)
                for t in range(TT):
                    dve.wait_ge(y_done, 2 + KF * N + KF)
                    nc.vector.scalar_tensor_tensor(out=xg[par][:, t, :], in0=ps_acc[t][:, :],
                                                   scalar=gate[:, 0, par:par + 1], in1=xg[par][:, t, :],
                                                   op0=ALU.mult, op1=ALU.add).then_inc(acc_free, 1)

            run(dve, window)

        @block.tensor
        def _(pe):
            def project_out(M, t):
                if t == 0:
                    pe.wait_ge(ctx_split, M + 1)
                    pe.wait_ge(x1_done, TT * M)
                for k in range(KD):
                    last = product3(pe, ps_p[t][:, :], [c[:, k, t * P:(t + 1) * P] for c in cts],
                                    [w[:, k, :] for w in wos], k == 0, k == KD - 1)
                last.then_inc(projected, 1)

            def transposes(M, first=False):
                pe.wait_ge(nrm_done, TT * M + TT)
                for k in range(KD):
                    if k >= 2 or not first:
                        pe.wait_ge(htf_done, KD * M + k - 1)
                    for t in range(TT):
                        last = pe.transpose(ps_tr[k % 2][:, t * P:(t + 1) * P], x1[:, t, k * P:(k + 1) * P], ident[:, :])
                    last.then_inc(tr_done, 1)

            pe.wait_ge(w_split, 2)
            for t in range(TT):
                project_out(0, t)
            pe.wait_ge(ident_made, 3)
            transposes(0, first=True)
            pe.wait_ge(w_split, len(pieces))

            def window(it, par, ahead, load):
                N = 2 * it + par

                def hidden(f):
                    if f == 0:
                        pe.wait_ge(ht_split, KD * N + KD)
                    pe.wait_ge(act_split, 2 + KF * N + f - 1)
                    for k in range(KD):
                        last = product3(pe, ps_h[f % 2][:, 0:T], [w[:, k, f * P:(f + 1) * P] for w in w1s],
                                        [h[:, k, :] for h in hts[par]], k == 0, k == KD - 1)
                    last.then_inc(h_done, 1)

                def output(f):
                    pe.wait_ge(act_split, 2 + KF * N + f + 1)
                    if f == 0:
                        pe.wait_ge(acc_free, TT * N)
                    for t in range(TT):
                        last = product3(pe, ps_acc[t][:, :], [a[:, t * P:(t + 1) * P] for a in acts[f % 2]],
                                        [w[:, f, :] for w in w2s], f == 0, f == KF - 1)
                    last.then_inc(y_done, 1)

                for f in range(KF):
                    hidden(f)
                    if f:
                        output(f - 1)
                    if ahead:
                        if PROJECT_AT <= f < PROJECT_AT + TT:
                            project_out(N + 1, f - PROJECT_AT)
                        if f == TURN_AT:
                            transposes(N + 1)
                output(KF - 1)

            run(pe, window)


def program(nc, x, xt, down_t, up_t, expert_t, cols, rows, ids, gates, wq, wk, wv, wo, w1, w2, out):
    x0_s = nc.dram_tensor("x0_scratch", (TOKENS, D), F32).ap()
    qk_s = nc.dram_tensor("qk_scratch", (2, D, 2, TOKENS), F32).ap()
    v_s = nc.dram_tensor("v_scratch", (TOKENS, D), F32).ap()
    ctx_s = nc.dram_tensor("ctx_scratch", (D, TOKENS), F32).ap()
    project(nc, x, xt, down_t, up_t, expert_t, cols, rows, ids, wq, wk, wv, x0_s, qk_s, v_s)
    attend(nc, qk_s, v_s, ctx_s)
    mlp(nc, ctx_s, x0_s, cols, rows, gates, wo, w1, w2, out)


def kernel(**inputs):
    import numpy as np
    import concourse.bacc as bacc
    from concourse.bass_utils import run_bass_kernel_spmd

    a = {k.replace("_cond", ""): np.asarray(v) for k, v in inputs.items()}
    x = a["x"].reshape(TOKENS, D)

    def column(v):
        return v.reshape(-1, P).T

    cols = np.concatenate([column(a["L0_down_b"]), a["L0_expert_b"].T, a["L0_domain_emb"].T,
                           column(a["L1_bq"]), column(a["L1_bk"]), column(a["L1_gamma1"]), column(a["L1_beta1"]),
                           column(a["L1_gamma2"]), column(a["L1_beta2"]), column(a["L1_b1"])], axis=1)
    rows = np.stack([a["L0_up_b"], a["L0_ln_gamma"], a["L0_ln_beta"], a["L1_bv"], a["L1_bo"], a["L1_b2"]])
    arrays = {
        "x": x, "xt": x.T, "down_t": a["L0_down_W"].T, "up_t": a["L0_up_W"].T,
        "expert_t": a["L0_expert_W"].transpose(2, 0, 1), "cols": cols,
        "rows": np.broadcast_to(rows[None], (P, *rows.shape)),
        "ids": np.broadcast_to(inputs["itok_B_0_15"], (P, BATCH)),
        "gates": np.broadcast_to(inputs["condB_gatescore"], (P, BATCH)),
        "wq": a["L1_Wq"], "wk": a["L1_Wk"], "wv": a["L1_Wv"], "wo": a["L1_Wo"], "w1": a["L1_W1"], "w2": a["L1_W2"],
    }
    arrays = {f"in_{k}": np.ascontiguousarray(v) for k, v in arrays.items()}
    nc = bacc.Bacc("TRN2", target_bir_lowering=False, num_devices=1)
    aps = {k[3:]: nc.dram_tensor(k, v.shape, mybir.dt.from_np(v.dtype), kind="ExternalInput").ap()
           for k, v in arrays.items()}
    out = nc.dram_tensor("out_0", (TOKENS, D), F32, kind="ExternalOutput").ap()
    program(nc, out=out, **aps)
    r = run_bass_kernel_spmd(nc, [arrays], core_ids=[0])
    return r.results[0]["out_0"].reshape(BATCH, SEQ, D)
```

```python
from contextlib import ExitStack

import concourse.bass as bass
from concourse import mybir

F32 = mybir.dt.float32
BF16 = mybir.dt.bfloat16
F32R = mybir.dt.float32r
I32 = mybir.dt.int32
ACT = mybir.ActivationFunctionType
ALU = mybir.AluOpType
AX = mybir.AxisListType

P = 128
BATCH, SEQ, D = 2, 2048, 512
TOKENS = BATCH * SEQ
KD = D // P
A, EXPERTS = 128, 16
HEADS, DH = 16, 32
F = 2048
KF = F // P
EPS = 1e-5
LOWEST = -3.0e38

C_DOWN_B = 0
C_EXPERT_B = C_DOWN_B + 1
C_EMB = C_EXPERT_B + EXPERTS
C_BQK = C_EMB + EXPERTS
C_G1 = C_BQK + 2 * KD
C_B1LN = C_G1 + KD
C_G2 = C_B1LN + KD
C_B2LN = C_G2 + KD
C_MLP_B1 = C_B2LN + KD
COLS = C_MLP_B1 + KF
R_UP_B, R_LN_G, R_LN_B, R_BV, R_BO, R_B2 = range(6)


def product3(pe, out, left, right, start, stop):
    pe.matmul(out, left[0], right[0], start=start, stop=False)
    pe.matmul(out, left[0], right[1], start=False, stop=False)
    return pe.matmul(out, left[1], right[0], start=False, stop=stop)


def stand_alone(eng, passed):
    eng.sem_inc(passed, 1)


def make_identity(pool, ident, made):
    pool.memset(ident, 0.0).then_inc(made, 1)
    pool.wait_ge(made, 1)
    pool.affine_select(out=ident, in_=ident, compare_op=ALU.not_equal, fill=1.0, base=0,
                       pattern=[[-1, P]], channel_multiplier=1).then_inc(made, 1)


def project(nc, x, xt, down_t, up_t, expert_t, cols, rows, ids, wq, wk, wv, x0_s, qk_s, v_s):
    T = 512
    TT = T // P
    PAIRS = SEQ // T
    RING = 4
    UNITS = 3 * KD
    PREP = 5 + BATCH * 3

    ctx = ExitStack()
    with ctx:
        def sb(name, shape, dt=F32):
            return ctx.enter_context(nc.sbuf_tensor(name, shape, dt))

        def sem(name):
            return ctx.enter_context(nc.semaphore(name))

        stage = [sb(f"stage{i}", [P, KD, T]) for i in range(2)]
        wqkv = [sb("wqkv_hi", [P, 3, KD, D], F32R), sb("wqkv_lo", [P, 3, KD, D], F32R)]
        wdown = [sb("wdown_hi", [P, KD, A], F32R), sb("wdown_lo", [P, KD, A], F32R)]
        wup = [sb("wup_hi", [P, D], F32R), sb("wup_lo", [P, D], F32R)]
        wexp_f = sb("wexp_f", [P, BATCH, A])
        weighted = sb("weighted", [P, A])
        wexp = [sb("wexp_hi", [P, BATCH, A], F32R), sb("wexp_lo", [P, BATCH, A], F32R)]
        col = sb("col_a", [P, COLS])
        row = sb("row_a", [P, 4, D])
        ident = sb("ident_a", [P, P])
        idsi = sb("idsi", [P, BATCH], I32)
        idf = sb("idf", [P, 4, BATCH])
        onehot = sb("onehot", [P, BATCH, EXPERTS])
        esel = sb("esel", [P, BATCH, 3, EXPERTS])
        bexp = sb("bexp", [P, 3, BATCH])
        xn = [sb(f"xn{i}", [P, TT, D]) for i in range(2)]
        xtf = sb("xtf", [P, KD, T])
        xts = [sb("xt_hi", [P, KD, T], F32R), sb("xt_lo", [P, KD, T], F32R)]
        hid = sb("hid", [P, T])
        hids = [sb("hid_hi", [P, T], F32R), sb("hid_lo", [P, T], F32R)]
        doms = [sb("dom_hi", [P, T], F32R), sb("dom_lo", [P, T], F32R)]
        nrm = sb("nrm", [P, TT, D])
        htf = [sb(f"htf{i}", [P, T]) for i in range(2)]
        hts = [[sb(f"ht_hi{i}", [P, KD, T], F32R), sb(f"ht_lo{i}", [P, KD, T], F32R)] for i in range(2)]
        experts = stage[1][:, :, :].rearrange("p k n -> p (k n)").rearrange("p (e o) -> p e o", e=EXPERTS)
        w_stage = [nrm[:, :, :], stage[0][:, :, :], stage[0][:, :, :]]
        qk_out = [sb(f"qk_out{i}", [P, 2, T], F32R) for i in range(RING)]
        v_out = [sb(f"v_out{i}", [P, D]) for i in range(2)]
        stats = sb("stats_a", [P, 2, TT, 6])
        mean_var = sb("mean_var_a", [P, 2, TT, 2])
        veps = sb("veps_a", [P, 2, TT])
        rstd = sb("rstd_a", [P, 2, TT])
        half = sb("half_a", [P, TT])
        ps_main = [ctx.enter_context(nc.psum_tensor(f"ps_main{i}", [P, T], F32)) for i in range(RING)]
        ps_mid = ctx.enter_context(nc.psum_tensor("ps_mid", [P, T], F32))
        ps_up = [ctx.enter_context(nc.psum_tensor(f"ps_up{i}", [P, D], F32)) for i in range(2)]
        ps_tr = ctx.enter_context(nc.psum_tensor("ps_tr", [P, T], F32))
        turned = [ps_mid, ps_up[0], ps_up[1], ps_tr]

        small_loaded = sem("small_loaded_a")
        rows_loaded = sem("rows_loaded_a")
        stage_loaded = [sem(f"stage_loaded{i}") for i in range(2)]
        w_loaded = [sem(f"wqkv_loaded{i}") for i in range(3)]
        stage_hi = sem("stage_hi")
        stage_split = sem("stage_split")
        w_hi = sem("wqkv_hi_done")
        w_split = sem("wqkv_split")
        selected = [sem(f"expert_selected{i}") for i in range(BATCH)]
        weighted_done = sem("weighted_done")
        wexp_hi = sem("wexp_hi_done")
        wexp_split = sem("wexp_split")
        prep = sem("prep_a")
        ident_made = sem("ident_made_a")
        passed = sem("passed_a")
        xn_loaded = [sem(f"xn_loaded{i}") for i in range(2)]
        xt_loaded = sem("xt_loaded")
        xt_hi = sem("xt_hi_done")
        xt_split = sem("xt_split")
        down_done = sem("down_done")
        gelu_done = sem("gelu_done_a")
        hid_hi = sem("hid_hi_done")
        hid_split = sem("hid_split")
        expert_done = sem("expert_done")
        dom_hi = sem("dom_hi_done")
        dom_split = sem("dom_split")
        biased = sem("biased_a")
        up_done = sem("up_done")
        y_done = sem("y_done")
        stats_done = sem("stats_done_a")
        aggr_done = sem("aggr_done_a")
        veps_done = sem("veps_done_a")
        rstd_done = sem("rstd_done_a")
        scaled = sem("scaled_a")
        x0_done = sem("x0_done")
        nrm_done = sem("nrm_done_a")
        x0_stored = [sem(f"x0_stored{i}") for i in range(2)]
        tr_done = sem("tr_done_a")
        htf_done = sem("htf_done_a")
        ht_hi = sem("ht_hi_done_a")
        ht_split = sem("ht_split_a")
        main_done = sem("main_done")
        qk_hi = sem("qk_hi_done")
        main_free = sem("main_free")
        qk_stored = [sem(f"qk_stored{i}") for i in range(RING)]
        v_stored = [sem(f"v_stored{i}") for i in range(2)]

        def run(eng, window):
            with eng.Fori(0, PAIRS - 1) as it:
                window(it, 0, True, True)
                window(it, 1, True, True)
            window(PAIRS - 1, 0, True, False)
            window(PAIRS - 1, 1, False, False)

        def after(it, par):
            return (it, 1) if par == 0 else (it + 1, 0)

        def tokens(it, par):
            return bass.ds(it * T + par * SEQ, T)

        block = ctx.enter_context(nc.Block())

        @block.sync
        def _(sp):
            sp.dma_start(stage[0][:, :, 0:A], down_t.rearrange("(k p) a -> p k a", p=P)).then_inc(stage_loaded[0], 16)
            sp.dma_start(stage[0][:, :, A:2 * A], up_t.rearrange("a (k n) -> a k n", k=KD)).then_inc(stage_loaded[0], 16)
            sp.dma_start(col[:, :], cols).then_inc(small_loaded, 16)
            sp.dma_start(idsi[:, :], ids).then_inc(small_loaded, 16)

            def load_xt(it, par):
                sp.dma_start(xtf[:, :, :], xt.rearrange("(k p) t -> p k t", p=P)[:, :, tokens(it, par)])\
                  .then_inc(xt_loaded, 16)

            def load_xn(it, par):
                sp.dma_start(xn[par][:, :, :], x[tokens(it, par), :].rearrange("(t p) d -> p t d", p=P))\
                  .then_inc(xn_loaded[par], 16)

            load_xt(0, 0)
            sp.dma_start(stage[1][:, :, :].rearrange("p k n -> p (k n)"),
                         expert_t.rearrange("a e o -> a (e o)")).then_inc(stage_loaded[1], 16)
            sp.dma_start(row[:, :, :], rows[:, 0:4, :]).then_inc(rows_loaded, 16)
            load_xn(0, 0)
            sp.dma_start(w_stage[0], wq.rearrange("(k p) n -> p k n", p=P)).then_inc(w_loaded[0], 16)
            sp.wait_ge(xt_split, 1)
            load_xt(0, 1)
            sp.wait_ge(stage_split, 1)
            sp.dma_start(w_stage[1], wk.rearrange("(k p) n -> p k n", p=P)).then_inc(w_loaded[1], 16)
            load_xn(0, 1)
            sp.wait_ge(w_split, 2)
            sp.dma_start(w_stage[2], wv.rearrange("(k p) n -> p k n", p=P)).then_inc(w_loaded[2], 16)

            def store_x0(it, par):
                N = 2 * it + par
                sp.wait_ge(x0_done, TT * N + TT)
                sp.dma_start(x0_s[tokens(it, par), :].rearrange("(t p) d -> p t d", p=P), xn[par][:, :, :])\
                  .then_inc(x0_stored[par], 16)

            def window(it, par, ahead, load):
                N = 2 * it + par
                if load:
                    sp.wait_ge(xt_split, N + 2)
                    stand_alone(sp, passed)
                    load_xt(it + 1, par)
                    sp.wait_ge(x0_stored[par], 16 * it + 16)
                    sp.wait_ge(nrm_done, TT * N + TT)
                    load_xn(it + 1, par)

                def store_qk(u):
                    sp.wait_ge(main_free, RING + UNITS * N + u + 1)
                    stand_alone(sp, passed)
                    sp.dma_start(qk_s[u // KD, (u % KD) * P:(u % KD + 1) * P, :, tokens(it, par)],
                                 qk_out[u % RING][:, :, :].bitcast(F32)).then_inc(qk_stored[u % RING], 16)

                def store_v(t):
                    sp.wait_ge(main_free, RING + UNITS * N + 2 * KD + t + 1)
                    sp.dma_start(v_s[bass.ds(it * T + par * SEQ + t * P, P), :], v_out[t % 2][:, :])\
                      .then_inc(v_stored[t % 2], 16)

                for u in range(2 * KD):
                    store_qk(u)
                store_v(0)
                store_v(1)
                if ahead:
                    store_x0(*after(it, par))
                store_v(2)
                store_v(3)

            store_x0(0, 0)
            run(sp, window)
            for par in range(2):
                sp.wait_ge(x0_stored[par], 16 * PAIRS)
                sp.wait_ge(v_stored[par], 16 * (2 * 2 * PAIRS + 1))
            for i in range(RING):
                sp.wait_ge(qk_stored[i], 16 * (2 * 2 * PAIRS + 1))

        @block.gpsimd
        def _(pool):
            make_identity(pool, ident[:, :], ident_made)
            pool.memset(half[:, :], -0.5).then_inc(ident_made, 1)
            pool.wait_ge(ident_made, 3)
            pool.wait_ge(rows_loaded, 16)

            def window(it, par, ahead, load):
                if not ahead:
                    return
                it, par = after(it, par)
                M = 2 * it + par
                adapter(it, par, M)

            def select(experts_from, experts_to):
                pool.wait_ge(stage_loaded[1], 16)
                pool.wait_ge(prep, PREP)
                for e in range(experts_from, experts_to):
                    pool.tensor_scalar(weighted[:, :], experts[:, e, :], esel[:, 1, 0, e:e + 1], None, ALU.mult)\
                        .then_inc(weighted_done, 1)
                    pool.wait_ge(weighted_done, e + 1)
                    pool.tensor_tensor(wexp_f[:, 1, :], wexp_f[:, 1, :], weighted[:, :], ALU.add)\
                        .then_inc(selected[1], 1)
                    pool.wait_ge(selected[1], e + 1)

            def adapter(it, par, M, first=False):
                if first:
                    select(0, 5)
                pool.wait_ge(xn_loaded[par], 16 * it + 16)
                for t in range(TT):
                    pool.tensor_tensor(xn[par][:, t, :], xn[par][:, t, :], row[:, R_UP_B, :], ALU.add).then_inc(biased, 1)
                for ln in range(2):
                    pool.wait_ge(veps_done, 2 * M + ln + 1)
                    pool.tensor_tensor(rstd[:, ln, :], veps[:, ln, :], half[:, :], ALU.pow).then_inc(rstd_done, 1)
                    if first:
                        select(*((5, 13), (13, EXPERTS))[ln])

            adapter(0, 0, 0, first=True)
            run(pool, window)

        @block.scalar
        def _(act):
            for i in range(RING):
                act.sem_inc(qk_stored[i], 16)
            act.wait_ge(small_loaded, 32)

            def xt_high(M):
                act.wait_ge(xt_loaded, 16 * M + 16)
                act.wait_ge(down_done, M)
                nc.scalar.activation(xts[0][:, :, :], xtf[:, :, :], ACT.Copy).then_inc(xt_hi, 1)

            def gelu(M):
                act.wait_ge(down_done, M + 1)
                act.wait_ge(hid_split, M)
                nc.scalar.activation(hid[:, :], ps_mid[:, :], ACT.Gelu, bias=col[:, C_DOWN_B:C_DOWN_B + 1])\
                  .then_inc(gelu_done, 1)
                act.wait_ge(expert_done, M)
                nc.scalar.activation(hids[0][:, :], ps_mid[:, :], ACT.Gelu, bias=col[:, C_DOWN_B:C_DOWN_B + 1])\
                  .then_inc(hid_hi, 1)

            def domain_hi(M, par):
                act.wait_ge(expert_done, M + 1)
                act.wait_ge(up_done, TT * M)
                nc.scalar.activation(doms[0][:, :], ps_mid[:, :], ACT.Identity, bias=bexp[:, 2, par:par + 1])\
                  .then_inc(dom_hi, 1)

            def affine(M, par, first=False):
                for k in range(KD):
                    act.wait_ge(tr_done, KD * M + k + 1)
                    if k >= 2 or not first:
                        act.wait_ge(ht_split, KD * M + k - 1)
                    for dst, done in ((htf[k % 2][:, :], htf_done), (hts[par][0][:, k, :], ht_hi)):
                        nc.scalar.activation(dst, turned[k][:, :], ACT.Identity, scale=col[:, C_G1 + k:C_G1 + k + 1],
                                             bias=col[:, C_B1LN + k:C_B1LN + k + 1]).then_inc(done, 1)

            def window(it, par, ahead, load):
                N = 2 * it + par
                M, mpar = N + 1, 1 - par

                def qk(u):
                    act.wait_ge(main_done, UNITS * N + u + 1)
                    act.wait_ge(qk_stored[u % RING], 16 * (2 * N + u // RING + 1))
                    nc.scalar.activation(qk_out[u % RING][:, 0, :], ps_main[u % RING][:, :], ACT.Identity,
                                         bias=col[:, C_BQK + u:C_BQK + u + 1]).then_inc(qk_hi, 1)

                if ahead:
                    gelu(M)
                qk(0)
                qk(1)
                if ahead:
                    domain_hi(M, mpar)
                for u in range(2, 2 * KD):
                    qk(u)
                if load:
                    xt_high(N + 2)
                if ahead:
                    affine(M, mpar)

            xt_high(0)
            act.wait_ge(prep, PREP)
            gelu(0)
            domain_hi(0, 0)

            def qkv_high(n):
                act.wait_ge(w_loaded[n], 16)
                nc.scalar.activation(wqkv[0][:, n, :, :], w_stage[n], ACT.Copy).then_inc(w_hi, 1)

            qkv_high(0)
            xt_high(1)
            qkv_high(1)
            affine(0, 0, first=True)
            qkv_high(2)
            run(act, window)

        @block.vector
        def _(dve):
            steps = [0]

            def step(ins):
                steps[0] += 1
                ins.then_inc(prep, 1)
                dve.wait_ge(prep, steps[0])

            for i in range(2):
                dve.sem_inc(v_stored[i], 16)
            nc.vector.memset(onehot[:, :, :], 0.0).then_inc(main_free, RING)
            dve.wait_ge(small_loaded, 32)
            dve.wait_ge(main_free, RING)
            step(nc.vector.tensor_copy(idf[:, 0, :], idsi[:, :]))
            step(nc.vector.tensor_scalar(idf[:, 1, :], idf[:, 0, :], 0.0, float(EXPERTS - 1), ALU.max, ALU.min))
            step(nc.vector.tensor_tensor(idf[:, 2, :], idf[:, 0, :], idf[:, 1, :], ALU.is_equal))
            step(nc.vector.tensor_scalar(idf[:, 3, :], idf[:, 2, :], -1.0, 1.0, ALU.mult, ALU.add))
            for e in range(EXPERTS):
                ins = nc.vector.tensor_scalar(onehot[:, :, e], idf[:, 1, :], float(e), None, ALU.is_equal)
            step(ins)
            dve.wait_ge(stage_loaded[0], 32)
            nc.vector.tensor_copy(wdown[0][:, :, :], stage[0][:, :, 0:A]).then_inc(stage_hi, 1)
            wup4 = [w[:, :].rearrange("p (k n) -> p k n", k=KD) for w in wup]
            nc.vector.tensor_copy(wup4[0], stage[0][:, :, A:2 * A]).then_inc(stage_hi, 1)
            dve.wait_ge(stage_hi, 2)
            nc.vector.tensor_tensor(wdown[1][:, :, :], stage[0][:, :, 0:A], wdown[0][:, :, :].bitcast(F32), ALU.subtract)\
              .then_inc(stage_hi, 1)
            nc.vector.tensor_tensor(wup4[1], stage[0][:, :, A:2 * A], wup4[0].bitcast(F32), ALU.subtract)\
              .then_inc(stage_split, 1)

            def xsplit(M):
                dve.wait_ge(xt_loaded, 16 * M + 16)
                dve.wait_ge(down_done, M)
                dve.wait_ge(xt_hi, M + 1)
                nc.vector.tensor_tensor(xts[1][:, :, :], xtf[:, :, :], xts[0][:, :, :].bitcast(F32), ALU.subtract)\
                  .then_inc(xt_split, 1)

            xsplit(0)
            dve.wait_ge(ident_made, 3)
            for b in range(BATCH):
                nc.vector.tensor_scalar(wexp_f[:, b, :], ident[:, :], idf[:, 3, b:b + 1], None, ALU.mult)
                step(nc.vector.tensor_scalar(esel[:, b, 0, :], onehot[:, b, :], idf[:, 2, b:b + 1], None, ALU.mult))
                nc.vector.tensor_tensor_reduce(esel[:, b, 1, :], col[:, C_EXPERT_B:C_EXPERT_B + EXPERTS],
                                               esel[:, b, 0, :], 1.0, 0.0, ALU.mult, ALU.add, bexp[:, 0, b:b + 1])
                step(nc.vector.tensor_tensor_reduce(esel[:, b, 2, :], col[:, C_EMB:C_EMB + EXPERTS],
                                                    onehot[:, b, :], 1.0, 0.0, ALU.mult, ALU.add, bexp[:, 1, b:b + 1]))
                step(nc.vector.tensor_tensor(bexp[:, 2, b:b + 1], bexp[:, 0, b:b + 1], bexp[:, 1, b:b + 1], ALU.add))
            assert steps[0] == PREP, steps[0]
            dve.wait_ge(stage_loaded[1], 16)
            for e in range(EXPERTS):
                nc.vector.scalar_tensor_tensor(out=wexp_f[:, 0, :], in0=experts[:, e, :], scalar=esel[:, 0, 0, e:e + 1],
                                               in1=wexp_f[:, 0, :], op0=ALU.mult, op1=ALU.add).then_inc(selected[0], 1)
                dve.wait_ge(selected[0], e + 1)

            def expert_split(b):
                dve.wait_ge(selected[b], EXPERTS)
                nc.vector.tensor_copy(wexp[0][:, b, :], wexp_f[:, b, :]).then_inc(wexp_hi, 1)
                dve.wait_ge(wexp_hi, b + 1)
                nc.vector.tensor_tensor(wexp[1][:, b, :], wexp_f[:, b, :], wexp[0][:, b, :].bitcast(F32), ALU.subtract)\
                  .then_inc(wexp_split, 1)

            def qkv_split(n):
                dve.wait_ge(w_hi, n + 1)
                nc.vector.tensor_tensor(wqkv[1][:, n, :, :], w_stage[n], wqkv[0][:, n, :, :].bitcast(F32), ALU.subtract)\
                  .then_inc(w_split, 1)

            expert_split(0)

            def hidden_split(M):
                dve.wait_ge(gelu_done, M + 1)
                dve.wait_ge(expert_done, M)
                dve.wait_ge(hid_hi, M + 1)
                nc.vector.tensor_tensor(hids[1][:, :], hid[:, :], hids[0][:, :].bitcast(F32), ALU.subtract)\
                  .then_inc(hid_split, 1)

            def domain_lo(M, par):
                dve.wait_ge(dom_hi, M + 1)
                nc.vector.scalar_tensor_tensor(out=doms[1][:, :], in0=ps_mid[:, :], scalar=bexp[:, 2, par:par + 1],
                                               in1=doms[0][:, :].bitcast(F32), op0=ALU.add, op1=ALU.subtract)\
                  .then_inc(dom_split, 1)

            def residual(M, par):
                for t in range(TT):
                    dve.wait_ge(up_done, TT * M + t + 1)
                    dve.wait_ge(biased, TT * M + t + 1)
                    nc.vector.tensor_tensor(xn[par][:, t, :], ps_up[t % 2][:, :], xn[par][:, t, :], ALU.add)\
                      .then_inc(y_done, 1)

            def statistics(M, par, ln, ready):
                for t in range(TT):
                    dve.wait_ge(ready, TT * M + t + 1)
                    if t == 0:
                        dve.wait_ge(rstd_done, 2 * M + ln)
                    nc.vector.bn_stats(stats[:, ln, t, :], xn[par][:, t, :]).then_inc(stats_done, 1)

            def variance(M, ln):
                dve.wait_ge(stats_done, TT * (2 * M + ln) + TT)
                stand_alone(dve, passed)
                for t in range(TT):
                    nc.vector.bn_aggr(mean_var[:, ln, t, :], stats[:, ln, t, :]).then_inc(aggr_done, 1)
                dve.wait_ge(aggr_done, TT * (2 * M + ln) + TT)
                nc.vector.tensor_scalar(veps[:, ln, :], mean_var[:, ln, :, 1], EPS, None, ALU.add).then_inc(veps_done, 1)

            def centre(M, par):
                for t in range(TT):
                    nc.vector.scalar_tensor_tensor(out=xn[par][:, t, :], in0=xn[par][:, t, :],
                                                   scalar=mean_var[:, 0, t, 0:1], in1=row[:, R_LN_G, :],
                                                   op0=ALU.subtract, op1=ALU.mult).then_inc(scaled, 1)

            def first_norm(M, par):
                dve.wait_ge(rstd_done, 2 * M + 1)
                for t in range(TT):
                    dve.wait_ge(scaled, TT * M + t + 1)
                    nc.vector.scalar_tensor_tensor(out=xn[par][:, t, :], in0=xn[par][:, t, :],
                                                   scalar=rstd[:, 0, t:t + 1], in1=row[:, R_LN_B, :],
                                                   op0=ALU.mult, op1=ALU.add).then_inc(x0_done, 1)

            def second_norm(M, par):
                dve.wait_ge(rstd_done, 2 * M + 2)
                dve.wait_ge(tr_done, KD * M)
                for t in range(TT):
                    nc.vector.tensor_scalar(nrm[:, t, :], xn[par][:, t, :], mean_var[:, 1, t, 0:1],
                                            rstd[:, 1, t:t + 1], ALU.subtract, ALU.mult).then_inc(nrm_done, 1)

            def h_split(M, par):
                for k in range(KD):
                    dve.wait_ge(ht_hi, KD * M + k + 1)
                    nc.vector.tensor_tensor(hts[par][1][:, k, :], htf[k % 2][:, :],
                                            hts[par][0][:, k, :].bitcast(F32), ALU.subtract).then_inc(ht_split, 1)

            hidden_split(0)
            domain_lo(0, 0)
            residual(0, 0)
            statistics(0, 0, 0, y_done)
            variance(0, 0)
            qkv_split(0)
            centre(0, 0)
            first_norm(0, 0)
            statistics(0, 0, 1, x0_done)
            variance(0, 1)
            xsplit(1)
            second_norm(0, 0)
            qkv_split(1)
            h_split(0, 0)
            expert_split(1)
            qkv_split(2)

            def window(it, par, ahead, load):
                N = 2 * it + par
                M = N + 1
                mpar = 1 - par

                def qk(u):
                    dve.wait_ge(qk_hi, 2 * KD * N + u + 1)
                    nc.vector.scalar_tensor_tensor(out=qk_out[u % RING][:, 1, :], in0=ps_main[u % RING][:, :],
                                                   scalar=col[:, C_BQK + u:C_BQK + u + 1],
                                                   in1=qk_out[u % RING][:, 0, :].bitcast(F32),
                                                   op0=ALU.add, op1=ALU.subtract).then_inc(main_free, 1)

                def v(t):
                    dve.wait_ge(main_done, UNITS * N + 2 * KD + t + 1)
                    dve.wait_ge(v_stored[t % 2], 16 * (2 * N + t // 2 + 1))
                    nc.vector.tensor_tensor(v_out[t % 2][:, :], ps_main[t % RING][:, :], row[:, R_BV, :], ALU.add)\
                      .then_inc(main_free, 1)

                if ahead:
                    hidden_split(M)
                qk(0)
                qk(1)
                if ahead:
                    domain_lo(M, mpar)
                qk(2)
                if ahead:
                    residual(M, mpar)
                if ahead:
                    statistics(M, mpar, 0, y_done)
                    variance(M, 0)
                qk(3)
                if ahead:
                    centre(M, mpar)
                qk(4)
                qk(5)
                if ahead:
                    first_norm(M, mpar)
                qk(6)
                if ahead:
                    statistics(M, mpar, 1, x0_done)
                    variance(M, 1)
                qk(7)
                if ahead:
                    second_norm(M, mpar)
                if load:
                    xsplit(N + 2)
                v(0)
                v(1)
                v(2)
                if ahead:
                    h_split(M, mpar)
                v(3)

            run(dve, window)

        @block.tensor
        def _(pe):
            def down(M, first=False):
                pe.wait_ge(xt_split, M + 1)
                if not first:
                    pe.wait_ge(ht_hi, KD * (M - 1) + 1)
                for k in range(KD):
                    last = product3(pe, ps_mid[:, :], [w[:, k, :] for w in wdown], [v[:, k, :] for v in xts],
                                    k == 0, k == KD - 1)
                last.then_inc(down_done, 1)

            def expert(M, par):
                pe.wait_ge(wexp_split, par + 1)
                pe.wait_ge(hid_split, M + 1)
                product3(pe, ps_mid[:, :], [w[:, par, :] for w in wexp], [v[:, :] for v in hids], True, True)\
                  .then_inc(expert_done, 1)

            def up(M):
                pe.wait_ge(dom_split, M + 1)
                for t in range(TT):
                    if t >= 2:
                        pe.wait_ge(y_done, TT * M + t - 1)
                    product3(pe, ps_up[t % 2][:, :], [v[:, t * P:(t + 1) * P] for v in doms],
                             [w[:, :] for w in wup], True, True).then_inc(up_done, 1)

            def transposes(M):
                pe.wait_ge(nrm_done, TT * M + TT)
                for k in range(KD):
                    for t in range(TT):
                        last = pe.transpose(turned[k][:, t * P:(t + 1) * P], nrm[:, t, k * P:(k + 1) * P], ident[:, :])
                    last.then_inc(tr_done, 1)

            def window(it, par, ahead, load):
                N = 2 * it + par
                M = N + 1

                def qk(u):
                    pe.wait_ge(main_free, UNITS * N + u + 1)
                    if u % KD == 0:
                        pe.wait_ge(w_split, u // KD + 1)
                    w = [z[:, u // KD, :, (u % KD) * P:(u % KD + 1) * P] for z in wqkv]
                    for k in range(KD):
                        if u == 0:
                            pe.wait_ge(ht_split, KD * N + k + 1)
                        last = product3(pe, ps_main[u % RING][:, :], [z[:, k, :] for z in w],
                                        [z[:, k, :] for z in hts[par]], k == 0, k == KD - 1)
                    last.then_inc(main_done, 1)

                def v(t):
                    pe.wait_ge(main_free, UNITS * N + 2 * KD + t + 1)
                    pe.wait_ge(w_split, 3)
                    for k in range(KD):
                        last = product3(pe, ps_main[t % RING][:, :], [z[:, k, t * P:(t + 1) * P] for z in hts[par]],
                                        [z[:, 2, k, :] for z in wqkv], k == 0, k == KD - 1)
                    last.then_inc(main_done, 1)

                if ahead:
                    down(M)
                qk(0)
                qk(1)
                if ahead:
                    expert(M, 1 - par)
                qk(2)
                if ahead:
                    up(M)
                for u in range(3, 2 * KD):
                    qk(u)
                v(0)
                v(1)
                v(2)
                if ahead:
                    transposes(M)
                v(3)

            pe.wait_ge(stage_split, 1)
            down(0, first=True)
            expert(0, 0)
            up(0)
            pe.wait_ge(ident_made, 3)
            transposes(0)
            run(pe, window)


def attend(nc, qk_s, v_s, ctx_s):
    QB = 512
    HG = 4
    NQ = SEQ // QB
    KT = SEQ // P
    PAIRS = HEADS // HG
    RING = 3
    SCORE_BANKS = 3
    ROWS, MROWS = 3 * DH, 3 * DH + 2
    SCALE = float(1.0 / DH ** 0.5)
    START, AHEAD = 52, 93
    TURN_LAG = 4
    QT = QB // P

    def scores(j):
        return [("s", j, h, q, c) for q in range(QT) for c in range(j + 1) for h in range(HG)]

    stream = scores(0)
    for j in range(1, NQ):
        more = scores(j)
        stream += more[:TURN_LAG] + [("t", j - 1)] + more[TURN_LAG:]
    UNITS = len(stream) + 1

    steps = [(j, k) for j in range(NQ) for k in range(QT * (j + 1))]
    STEPS = len(steps)

    def offset(j, k):
        return max(0, k - QT * j) * P

    def paired(n):
        return steps[n][1] < QT * steps[n][0] + 2

    pairs = [n for n in range(STEPS) if paired(n) and steps[n][1] % 2 == 0]
    BUFFER = [n % 3 for n in range(STEPS - 1)] + [1]

    def used_by_pair(n):
        before = [m for m in range(n) if BUFFER[m] == BUFFER[n]]
        return [p for p, m in enumerate(pairs) if before and before[-1] in (m, m + 1)]

    def shares(first, last):
        own = [(False, u) for u in stream[START if first else AHEAD:]]
        nxt = [(True, u) for u in stream[:AHEAD]]
        units = own + nxt[:TURN_LAG] + [(False, ("t", NQ - 1))] + nxt[TURN_LAG:]
        work = [QB - offset(*s) + 200 for s in steps]
        total, done, out, at = sum(work), 0, [], 0
        for n, w in enumerate(work):
            done += w
            upto = len(units) * done // total
            for j in range(NQ):
                if n + 3 > steps.index((j, 0)) and (False, ("t", j)) in units:
                    upto = max(upto, units.index((False, ("t", j))) + 1)
            out.append([u for u in units[at:upto] if not (last and u[0])])
            at = upto
        return out

    ctx = ExitStack()
    with ctx:
        def sb(name, shape, dt=F32):
            return ctx.enter_context(nc.sbuf_tensor(name, shape, dt))

        def sem(name):
            return ctx.enter_context(nc.semaphore(name))

        qs = [sb(f"q_stack{i}", [P, NQ, HG, QB], F32R) for i in range(2)]
        ks = [sb(f"k_stack{i}", [P, HG, SEQ], F32R) for i in range(2)]
        vt = [sb(f"v_tiles{i}", [P, KT, HG * DH]) for i in range(2)]
        probs = [sb(f"probs{i}", [P, HG, QB]) for i in range(3)]
        pair = [sb(f"pair{i}", [P, HG, QB]) for i in range(2)]
        ident = sb("ident_b", [P, P])
        ones = sb("ones_b", [P, DH])
        mask = sb("mask_b", [P, QB])
        causal_f = sb("causal_f", [P, P])
        causal = sb("causal", [P, P], BF16)
        ident_h = sb("ident_h", [P, P], BF16)
        junk = sb("junk_b", [P, RING, QB], BF16)
        mpart = sb("mpart", [P, 2, HG * QT, NQ])
        mrow = sb("mrow", [P, 2, 2, HG * QT])
        mhi = sb("mhi", [P, 2, HG * QT], F32R)
        mcol = sb("mcol", [P, 2, 2, HG * QT])
        mturn = sb("mturn", [2 * HG * QT, 2, P])
        o_sb = sb("o_sb", [P, QB])
        sum_t = sb("sum_t", [P, QB // DH, DH])
        rec = sb("rec", [P, QB // DH])
        rec_t = sb("rec_t", [P, QB // DH, DH])
        rec_b = sb("rec_b", [P, QB])
        cx = sb("cx", [P, 2, QB])
        ps_m = [ctx.enter_context(nc.psum_tensor(f"ps_m{i}", [P, QB], F32)) for i in range(RING)]
        ps_s = [ctx.enter_context(nc.psum_tensor(f"ps_s{i}", [P, QB], F32)) for i in range(SCORE_BANKS)]
        ps_o = ctx.enter_context(nc.psum_tensor("ps_o", [P, QB], F32))
        ps_sum = ctx.enter_context(nc.psum_tensor("ps_sum", [P, QB], F32))

        consts = sem("consts_b")
        half_consts = sem("half_consts")
        ones_made = sem("ones_made")
        passed = sem("passed_b")
        loaded = [[sem(f"stacks{i}_loaded{j}") for j in range(NQ)] for i in range(2)]
        unit_done = sem("unit_done")
        unit_free = sem("unit_free")
        max_done = sem("max_done")
        neg_done = sem("neg_done")
        mhi_done = sem("mhi_done")
        mcol_done = sem("mcol_done")
        m_stacked = [sem(f"m_stacked{i}") for i in range(2)]
        s_done = sem("s_done")
        exp_done = sem("exp_done")
        added = sem("added")
        copied = sem("copied")
        pv_done = sem("pv_done")
        sum_turned = sem("sum_turned")
        o_taken = sem("o_taken")
        rec_done = sem("rec_done")
        rec_spread = sem("rec_spread")
        rec_turned = sem("rec_turned")
        ctx_done = sem("ctx_done")
        ctx_stored = [sem(f"ctx_stored{i}") for i in range(2)]

        def run(eng, window):
            window(0, 0, True, False)
            with eng.Fori(0, PAIRS - 1) as it:
                window(it, 1, False, False)
                window(it + 1, 0, False, False)
            window(PAIRS - 1, 1, False, True)

        def is_first(n):
            return isinstance(n, int) and n == 0

        def behind(it, par):
            return (it, 1) if par == 0 else (it + 1, 0)

        def before(it, par):
            return (it, 0) if par == 1 else (it - 1, 1)

        def numbered(it, par, first, last):
            base = 0 if first else UNITS * (2 * it + par) + AHEAD
            i = START if first else 0
            out = []
            for share in shares(first, last):
                out.append([(*(behind(it, par) if nxt else (it, par)), u, base, i + n) for n, (nxt, u) in enumerate(share)])
                i += len(share)
            return out

        block = ctx.enter_context(nc.Block())

        @block.sync
        def _(sp):
            def load(it, par):
                for j in range(NQ):
                    block_j = slice(par * SEQ + j * QB, par * SEQ + (j + 1) * QB)
                    for r, part in enumerate((0, 1, 0)):
                        sp.dma_start(ks[par][r * DH:(r + 1) * DH, :, j * QB:(j + 1) * QB].bitcast(F32),
                                     qk_s[1, bass.ds(it * P, P), part, block_j].rearrange("(h p) t -> p h t", p=DH))\
                          .then_inc(loaded[par][j], 16)
                    for r, part in enumerate((0, 0, 1)):
                        sp.dma_start(qs[par][r * DH:(r + 1) * DH, j, :, :].bitcast(F32),
                                     qk_s[0, bass.ds(it * P, P), part, block_j].rearrange("(h p) t -> p h t", p=DH))\
                          .then_inc(loaded[par][j], 16)
                    sp.dma_start(vt[par][:, j * QT:(j + 1) * QT, :],
                                 v_s[block_j, bass.ds(it * P, P)].rearrange("(t p) d -> p t d", p=P))\
                      .then_inc(loaded[par][j], 16)

            def stack_max(it, par, j, index):
                sp.wait_ge(unit_free, index + 1)
                for part in range(2):
                    sp.dma_start(qs[par][ROWS + part:ROWS + part + 1, j, :, :].rearrange("p h t -> p (h t)").bitcast(F32),
                                 mturn[part * HG * QT:(part + 1) * HG * QT, j % 2, :])\
                      .then_inc(m_stacked[j % 2], 16)

            def store(it, par, j):
                sp.wait_ge(ctx_done, NQ * (2 * it + par) + j + 1)
                stand_alone(sp, passed)
                sp.dma_start(ctx_s[bass.ds(it * P, P), par * SEQ + j * QB:par * SEQ + (j + 1) * QB],
                             cx[:, j % 2, :]).then_inc(ctx_stored[j % 2], 16)

            def window(it, par, first, last):
                W = 2 * it + par
                share = numbered(it, par, first, last)

                def maxima(n):
                    for uit, upar, u, base, i in share[n]:
                        if u[0] == "t":
                            stack_max(uit, upar, u[1], base + i)

                maxima(0)
                if not first:
                    store(*before(it, par), NQ - 1)
                if not last:
                    if not first:
                        sp.wait_ge(pv_done, STEPS * W)
                        stand_alone(sp, passed)
                    load(*behind(it, par))
                for n in range(1, STEPS):
                    maxima(n)
                    if steps[n - 1][1] == 0 and n > 1:
                        store(it, par, steps[n - 1][0] - 1)
                if last:
                    store(it, par, NQ - 1)

            load(0, 0)
            for i, u in enumerate(stream[:START]):
                if u[0] == "t":
                    stack_max(0, 0, u[1], i)
            run(sp, window)
            for i in range(2):
                sp.wait_ge(ctx_stored[i], 16 * (2 * PAIRS * NQ // 2))

        @block.gpsimd
        def _(pool):
            make_identity(pool, ident[:, :], consts)
            pool.memset(mask[:, :], 0.0).then_inc(consts, 1)
            pool.wait_ge(consts, 3)
            pool.affine_select(out=mask[:, QB - P:], in_=mask[:, QB - P:], compare_op=ALU.is_ge, fill=LOWEST, base=0,
                               pattern=[[-1, P]], channel_multiplier=1).then_inc(consts, 1)
            pool.memset(causal_f[:, :], 0.0).then_inc(consts, 1)
            pool.wait_ge(consts, 5)
            pool.affine_select(out=causal_f[:, :], in_=causal_f[:, :], compare_op=ALU.is_ge, fill=-1.0e30, base=0,
                               pattern=[[1, P]], channel_multiplier=-1).then_inc(consts, 1)
            pool.memset(ones[:, :], 1.0).then_inc(ones_made, 1)
            for i in range(2):
                pool.wait_ge(ones_made, i + 1)
                pool.memset(ks[i][ROWS:MROWS, :, :].bitcast(F32), 1.0).then_inc(ones_made, 1)

            pool.wait_ge(ones_made, 3)

            def sums_made(p):
                return pairs[p] + 3 if p >= 0 else pairs[p] + 3 - STEPS

            def divide(it, par, j):
                B = NQ * (2 * it + par) + j
                pool.wait_ge(rec_turned, B + 1)
                pool.wait_ge(o_taken, B + 1)
                if j >= 2 or not is_first(it) or par:
                    pool.wait_ge(ctx_stored[j % 2], 16 * (2 * (2 * it + par) + j // 2))
                pool.tensor_tensor(cx[:, j % 2, :], o_sb[:, :], rec_b[:, :], ALU.mult).then_inc(ctx_done, 1)

            def window(it, par, first, last):
                W = 2 * it + par
                for p, n in enumerate(pairs):
                    j = steps[n][0]
                    off = offset(*steps[n + 1])
                    if off:
                        if not (first and p < 2):
                            pool.wait_ge(pv_done, STEPS * W + sums_made(p - 2))
                        pool.wait_ge(exp_done, HG * (STEPS * W + n + 1))
                        stand_alone(pool, passed)
                        pool.tensor_copy(pair[p % 2][:, :, 0:off], probs[BUFFER[n]][:, :, 0:off]).then_inc(copied, 1)
                    for h in range(HG):
                        if not (first and p < 2):
                            pool.wait_ge(pv_done, STEPS * W + sums_made(p - 2))
                        pool.wait_ge(exp_done, HG * (STEPS * W + n + 1) + h + 1)
                        pool.tensor_tensor(pair[p % 2][:, h, off:], probs[BUFFER[n]][:, h, off:],
                                           probs[BUFFER[n + 1]][:, h, off:], ALU.add).then_inc(added, 1)
                    if p == 0 and not first:
                        divide(*before(it, par), NQ - 1)
                    if steps[n][1] == 2:
                        divide(it, par, j - 1)
                if last:
                    divide(it, par, NQ - 1)

            run(pool, window)

        @block.scalar
        def _(act):
            def take_values(it, par, j):
                B = NQ * (2 * it + par) + j
                done = sum(1 for s in steps if s[0] <= j)
                act.wait_ge(pv_done, STEPS * (2 * it + par) + done)
                if not (is_first(it) and par == 0 and j == 0):
                    act.wait_ge(ctx_done, B)
                nc.scalar.activation(o_sb[:, :], ps_o[:, :], ACT.Copy).then_inc(o_taken, 1)

            def window(it, par, first, last):
                G = STEPS * (2 * it + par)
                for n, (j, k) in enumerate(steps):
                    off = offset(j, k)
                    for h in range(HG):
                        act.wait_ge(s_done, HG * (G + n) + h + 1)
                        for p in used_by_pair(n) + ([-1] if n == 0 and not first else []):
                            act.wait_ge(added, HG * (len(pairs) * (2 * it + par) + p) + h + 1)
                        nc.scalar.activation(probs[BUFFER[n]][:, h, off:], ps_s[(HG * n + h) % SCORE_BANKS][:, off:],
                                             ACT.Exp, scale=SCALE).then_inc(exp_done, 1)
                    if n == 0 and not first:
                        take_values(*before(it, par), NQ - 1)
                    if n and k == 0:
                        take_values(it, par, j - 1)
                if last:
                    take_values(it, par, NQ - 1)

            run(act, window)

        @block.vector
        def _(dve):
            dve.wait_ge(consts, 6)
            nc.vector.tensor_copy(causal[:, :], causal_f[:, :]).then_inc(half_consts, 1)
            nc.vector.tensor_copy(ident_h[:, :], ident[:, :]).then_inc(half_consts, 1)

            def unit(it, par, u, index, slot):
                W = 2 * it + par
                dve.wait_ge(unit_done, index + 1)
                if u[0] == "t":
                    j = u[1]
                    before = 32 * (2 * W + j // 2)
                    dve.wait_ge(m_stacked[j % 2], before)
                    nc.vector.tensor_copy(mturn[:, j % 2, :], ps_m[slot][0:2 * HG * QT, 0:P]).then_inc(unit_free, 1)
                    return
                _, j, h, q, c = u
                out = mpart[:, j % 2, h * QT + q, c:c + 1]
                if c < j:
                    nc.vector.tensor_reduce(out, ps_m[slot][:, :], AX.X, ALU.max).then_inc(unit_free, 1)
                else:
                    stand_alone(dve, passed)
                    w = (q + 1) * P
                    nc.vector.tensor_tensor_reduce(junk[:, slot, 0:w], ps_m[slot][:, 0:w], mask[:, QB - w:], 1.0, LOWEST,
                                                   ALU.add, ALU.max, out).then_inc(unit_free, 1)

            def finish_max(it, par, j, index):
                B = NQ * (2 * it + par) + j
                b = j % 2
                dve.wait_ge(unit_free, index + 1)
                nc.vector.tensor_reduce(mrow[:, b, 0, :], mpart[:, b, :, 0:j + 1], AX.X, ALU.max).then_inc(max_done, 1)
                dve.wait_ge(max_done, B + 1)
                nc.vector.tensor_scalar(mrow[:, b, 1, :], mrow[:, b, 0, :], -1.0, None, ALU.mult).then_inc(neg_done, 1)
                dve.wait_ge(neg_done, B + 1)
                nc.vector.tensor_copy(mhi[:, b, :], mrow[:, b, 1, :]).then_inc(mhi_done, 1)
                dve.wait_ge(mhi_done, B + 1)
                nc.vector.tensor_copy(mcol[:, b, 0, :], mhi[:, b, :].bitcast(F32)).then_inc(mcol_done, 1)
                nc.vector.tensor_tensor(mcol[:, b, 1, :], mrow[:, b, 1, :], mhi[:, b, :].bitcast(F32), ALU.subtract)\
                  .then_inc(mcol_done, 1)

            def take_sums(it, par, j):
                done = sum(1 for s in steps if s[0] <= j)
                dve.wait_ge(pv_done, STEPS * (2 * it + par) + done)
                nc.vector.transpose(sum_t[:, :, :].rearrange("p c i -> p (c i)"), ps_sum[:, :]).then_inc(sum_turned, 1)

            def invert(it, par, j):
                B = NQ * (2 * it + par) + j
                dve.wait_ge(sum_turned, B + 1)
                nc.vector.reciprocal(rec[:, :], sum_t[:, :, 0]).then_inc(rec_done, 1)

            def spread(it, par, j):
                B = NQ * (2 * it + par) + j
                dve.wait_ge(rec_done, B + 1)
                nc.vector.tensor_copy(rec_t[:, :, :], rec[:, :].unsqueeze(2).to_broadcast([P, QB // DH, DH]))\
                  .then_inc(rec_spread, 1)

            def turn_back(it, par, j):
                B = NQ * (2 * it + par) + j
                dve.wait_ge(rec_spread, B + 1)
                if not (is_first(it) and par == 0 and j == 0):
                    dve.wait_ge(ctx_done, B)
                nc.vector.transpose(rec_b[:, :], rec_t[:, :, :].rearrange("p c i -> p (c i)")).then_inc(rec_turned, 1)

            def last_of(u):
                return u[0] == "s" and u == scores(u[1])[-1]

            def do(it, par, u, base, i):
                unit(it, par, u, base + i, i % RING)
                if last_of(u):
                    finish_max(it, par, u[1], base + i)

            for i, u in enumerate(stream[:START]):
                do(0, 0, u, 0, i)

            def window(it, par, first, last):
                share = numbered(it, par, first, last)

                def with_units(n, bit, bpar, j):
                    todo = share[n]
                    for i, stage in enumerate((invert, spread, turn_back)):
                        if i < len(todo):
                            do(*todo[i])
                        stage(bit, bpar, j)
                    for u in todo[3:]:
                        do(*u)

                for n in range(STEPS):
                    if n == 1 and not first:
                        with_units(n, *before(it, par), NQ - 1)
                    elif n > 1 and steps[n - 1][1] == 0:
                        with_units(n, it, par, steps[n - 1][0] - 1)
                    else:
                        for u in share[n]:
                            do(*u)
                    if n == 0 and not first:
                        take_sums(*before(it, par), NQ - 1)
                    if n and steps[n][1] == 0:
                        take_sums(it, par, steps[n][0] - 1)
                if last:
                    take_sums(it, par, NQ - 1)
                    for stage in (invert, spread, turn_back):
                        stage(it, par, NQ - 1)

            run(dve, window)

        @block.tensor
        def _(pe):
            pe.wait_ge(consts, 6)
            pe.wait_ge(half_consts, 2)

            def unit(it, par, u, base, i):
                if not is_first(base) or i >= RING:
                    pe.wait_ge(unit_free, base + i - (RING - 1 if i >= 2 else 1))
                ps = ps_m[i % RING]
                if u[0] == "t":
                    j = u[1]
                    pe.wait_ge(mcol_done, 2 * (NQ * (2 * it + par) + j) + 2)
                    pe.transpose(ps[0:2 * HG * QT, 0:P], mcol[:, j % 2, :, :].rearrange("p a n -> p (a n)"),
                                 ident[:, :]).then_inc(unit_done, 1)
                    return
                _, j, h, q, c = u
                if u == scores(j)[0]:
                    pe.wait_ge(loaded[par][j], 16 * 7 * (it + 1))
                w = QB if c < j else (q + 1) * P
                pe.matmul(ps[:, 0:w], qs[par][0:ROWS, j, h, q * P:(q + 1) * P], ks[par][0:ROWS, h, c * QB:c * QB + w],
                          start=True, stop=True).then_inc(unit_done, 1)

            for i, u in enumerate(stream[:START]):
                unit(0, 0, u, 0, i)

            def window(it, par, first, last):
                W = 2 * it + par
                G = STEPS * W

                def probabilities(n, h):
                    j, k = steps[n]
                    off = offset(j, k)
                    if k == 0 and h == 0:
                        pe.wait_ge(m_stacked[j % 2], 32 * (2 * W + j // 2 + 1))
                    if n or h >= SCORE_BANKS:
                        pe.wait_ge(exp_done, HG * (G + n) + h - SCORE_BANKS + 1)
                    elif h == 0 and not first:
                        pe.wait_ge(exp_done, HG * G)
                    ps = ps_s[(HG * n + h) % SCORE_BANKS]
                    mm = pe.matmul(ps[:, off:], ks[par][0:MROWS, h, k * P:(k + 1) * P],
                                   qs[par][0:MROWS, j, h, off:], start=True, stop=k < QT * j)
                    if k >= QT * j:
                        mm = pe.matmul(ps[:, off:off + P], ident_h[:, :], causal[:, :], start=False, stop=True)
                    mm.then_inc(s_done, 1)

                def weigh(wpar, W, n):
                    j, k = steps[n]
                    off = offset(j, k)
                    if k == 0 and not (is_first(W) and j == 0):
                        pe.wait_ge(o_taken, NQ * W + j)
                        pe.wait_ge(sum_turned, NQ * W + j)
                    for h in range(HG):
                        mm = pe.matmul(ps_o[h * DH:(h + 1) * DH, off:], vt[wpar][:, k, h * DH:(h + 1) * DH],
                                       probs[BUFFER[n]][:, h, off:], start=(k == 0), stop=(k == QT * (j + 1) - 1))
                    if n and paired(n - 1) and k and k % 2 == 0:
                        p = pairs.index(n - 2)
                        pe.wait_ge(added, HG * (len(pairs) * W + p + 1))
                        if k > QT * j:
                            pe.wait_ge(copied, NQ * W + j + 1)
                        for h in range(HG):
                            mm = pe.matmul(ps_sum[h * DH:(h + 1) * DH, :], ones[:, :], pair[p % 2][:, h, :],
                                           start=(k == 2), stop=False)
                    if not paired(n):
                        for h in range(HG):
                            mm = pe.matmul(ps_sum[h * DH:(h + 1) * DH, off:], ones[:, :], probs[BUFFER[n]][:, h, off:],
                                           start=(k == 0), stop=(k == QT * (j + 1) - 1))
                    mm.then_inc(pv_done, 1)

                for n, share in enumerate(numbered(it, par, first, last)):
                    for h in range(HG):
                        probabilities(n, h)
                        if h < len(share):
                            unit(*share[h])
                    if n:
                        pe.wait_ge(exp_done, HG * (G + n))
                        weigh(par, W, n - 1)
                    elif not first:
                        weigh(1 - par, W - 1, STEPS - 1)
                    for u in share[HG:]:
                        unit(*u)
                if last:
                    pe.wait_ge(exp_done, HG * (G + STEPS))
                    weigh(par, W, STEPS - 1)

            pe.wait_ge(ones_made, 3)
            run(pe, window)


def mlp(nc, ctx_s, x0_s, cols, rows, gates, wo, w1, w2, out):
    T = 256
    TT = T // P
    PAIRS = SEQ // T
    STAGES = 4
    BLOCKS = 1
    LEAD = 4
    PROJECT_AT, TURN_AT = 3, 12

    ctx = ExitStack()
    with ctx:
        def sb(name, shape, dt=F32):
            return ctx.enter_context(nc.sbuf_tensor(name, shape, dt))

        def sem(name):
            return ctx.enter_context(nc.semaphore(name))

        w1s = [sb("w1_hi", [P, KD, F], F32R), sb("w1_lo", [P, KD, F], F32R)]
        w2s = [sb("w2_hi", [P, KF, D], F32R), sb("w2_lo", [P, KF, D], F32R)]
        wos = [sb("wo_hi", [P, KD, D], F32R), sb("wo_lo", [P, KD, D], F32R)]
        col = sb("col_c", [P, COLS])
        bo = sb("bo_row", [P, D])
        gb2 = sb("gb2", [P, BATCH, D])
        gate = sb("gate", [P, 2, BATCH])
        ident = sb("ident_c", [P, P])
        half = sb("half_c", [P, TT])
        stage = [sb(f"w_stage{i}", [P, BLOCKS * D]) for i in range(STAGES)]
        xg = [sb(f"xg{i}", [P, TT, D]) for i in range(2)]
        x1 = sb("x1", [P, TT, D])
        cf = sb("cf", [P, KD, T])
        cts = [sb("ct_hi", [P, KD, T], F32R), sb("ct_lo", [P, KD, T], F32R)]
        htf = [sb(f"h2f{i}", [P, T]) for i in range(2)]
        hts = [[sb(f"h2_hi{i}", [P, KD, T], F32R), sb(f"h2_lo{i}", [P, KD, T], F32R)] for i in range(2)]
        act_f = [sb(f"act_f{i}", [P, T]) for i in range(2)]
        acts = [[sb(f"act_hi{i}", [P, T], F32R), sb(f"act_lo{i}", [P, T], F32R)] for i in range(2)]
        stats = sb("stats_c", [P, TT, 6])
        mean_var = sb("mean_var_c", [P, TT, 2])
        veps = sb("veps_c", [P, TT])
        rstd = sb("rstd_c", [P, TT])
        ps_acc = [ctx.enter_context(nc.psum_tensor(f"ps_acc{i}", [P, D], F32)) for i in range(TT)]
        ps_h = [ctx.enter_context(nc.psum_tensor(f"ps_h{i}", [P, 512], F32)) for i in range(2)]
        ps_p = [ctx.enter_context(nc.psum_tensor(f"ps_p{i}", [P, D], F32)) for i in range(TT)]
        ps_tr = [ctx.enter_context(nc.psum_tensor(f"ps_tr_c{i}", [P, 512], F32)) for i in range(2)]

        small_loaded = sem("small_loaded_c")
        bo_loaded = sem("bo_loaded")
        col_loaded = sem("col_loaded_c")
        ident_made = sem("ident_made_c")
        passed = sem("passed_c")
        w_loaded = [sem(f"w_loaded{i}") for i in range(STAGES)]
        w_hi = sem("w_hi")
        w_split = sem("w_split")
        prep = sem("prep_c")
        xg_loaded = [sem(f"xg_loaded{i}") for i in range(2)]
        ctx_loaded = sem("ctx_loaded")
        ctx_hi = sem("ctx_hi")
        ctx_split = sem("ctx_split")
        with_bo = sem("with_bo")
        kept = sem("kept")
        kept_b = sem("kept_b")
        projected = sem("projected")
        x1_done = sem("x1_done")
        stats_done = sem("stats_done_c")
        aggr_done = sem("aggr_done_c")
        veps_done = sem("veps_done_c")
        rstd_done = sem("rstd_done_c")
        z_done = sem("z_done")
        nrm_done = sem("nrm_done_c")
        tr_done = sem("tr_done_c")
        htf_done = sem("htf_done_c")
        ht_hi = sem("ht_hi_done_c")
        ht_split = sem("ht_split_c")
        h_done = sem("h_done")
        gelu_done = sem("gelu_done_c")
        act_hi = sem("act_hi")
        act_split = sem("act_split")
        y_done = sem("y_done_c")
        acc_free = sem("acc_free")
        out_stored = [sem(f"out_stored{i}") for i in range(2)]

        WO_PIECES = KD // BLOCKS
        pieces = []
        for n in range(WO_PIECES):
            pieces.append((wo[n * BLOCKS * P:(n + 1) * BLOCKS * P, :].rearrange("(k p) n -> p k n", p=P),
                           [w[:, n * BLOCKS:(n + 1) * BLOCKS, :] for w in wos]))
        for n in range(KF // BLOCKS):
            features = slice(n * BLOCKS * P, (n + 1) * BLOCKS * P)
            pieces.append((w1[:, features].rearrange("(k p) n -> p k n", p=P), [w[:, :, features] for w in w1s]))
            pieces.append((w2[features, :].rearrange("(k p) n -> p k n", p=P),
                           [w[:, n * BLOCKS:(n + 1) * BLOCKS, :] for w in w2s]))

        def staged(n):
            return stage[n % STAGES][:, :].rearrange("p (k n) -> p k n", k=pieces[n][0].shape[1])

        def pieces_for(f):
            n = f // BLOCKS + LEAD
            at = WO_PIECES + 2 * n
            return (at, at + 1) if f % BLOCKS == 0 and at < len(pieces) else ()

        def run(eng, window):
            window(0, 0, True, True, first=True)
            window(0, 1, True, True)
            with eng.Fori(1, PAIRS - 1) as it:
                window(it, 0, True, True)
                window(it, 1, True, True)
            window(PAIRS - 1, 0, True, False)
            window(PAIRS - 1, 1, False, False)

        def tokens(it, par):
            return bass.ds(it * T + par * SEQ, T)

        block = ctx.enter_context(nc.Block())

        @block.sync
        def _(sp):
            def load_ctx(it, par):
                sp.dma_start(cf[:, :, :], ctx_s.rearrange("(k p) t -> p k t", p=P)[:, :, tokens(it, par)])\
                  .then_inc(ctx_loaded, 16)

            def load_x(it, par):
                sp.dma_start(xg[par][:, :, :], x0_s[tokens(it, par), :].rearrange("(t p) d -> p t d", p=P))\
                  .then_inc(xg_loaded[par], 16)

            def load_piece(n):
                if n >= STAGES:
                    sp.wait_ge(w_split, n + 1 - STAGES)
                sp.dma_start(staged(n), pieces[n][0]).then_inc(w_loaded[n % STAGES], 16)

            load_ctx(0, 0)
            for n in range(WO_PIECES):
                load_piece(n)
            load_x(0, 0)
            sp.dma_start(bo[:, :], rows[:, R_BO, :]).then_inc(bo_loaded, 16)
            sp.dma_start(gate[:, 0, :], gates).then_inc(small_loaded, 16)
            for b in range(BATCH):
                sp.dma_start(gb2[:, b, :], rows[:, R_B2, :]).then_inc(small_loaded, 16)
            sp.dma_start(col[:, :], cols).then_inc(col_loaded, 16)
            for n in range(WO_PIECES, len(pieces)):
                load_piece(n)
                if n == WO_PIECES + 4:
                    sp.wait_ge(ctx_split, 1)
                    load_ctx(0, 1)
                    load_x(0, 1)

            def window(it, par, ahead, load, first=False):
                N = 2 * it + par
                if load:
                    sp.wait_ge(ctx_split, N + 2)
                    stand_alone(sp, passed)
                    load_ctx(it + 1, par)
                sp.wait_ge(acc_free, TT * N + TT + 1)
                stand_alone(sp, passed)
                sp.dma_start(out[tokens(it, par), :].rearrange("(t p) d -> p t d", p=P), xg[par][:, :, :])\
                  .then_inc(out_stored[par], 16)
                if load:
                    sp.wait_ge(out_stored[par], 16 * it + 16)
                    load_x(it + 1, par)

            run(sp, window)
            for par in range(2):
                sp.wait_ge(out_stored[par], 16 * PAIRS)

        @block.gpsimd
        def _(pool):
            make_identity(pool, ident[:, :], ident_made)
            pool.memset(half[:, :], -0.5).then_inc(ident_made, 1)
            pool.wait_ge(ident_made, 3)
            pool.wait_ge(bo_loaded, 16)

            def chunk(it, par, M, first=False):
                pool.wait_ge(xg_loaded[par], 16 * it + 16)
                pool.wait_ge(tr_done, KD * M)
                for t in range(TT):
                    pool.tensor_tensor(x1[:, t, :], xg[par][:, t, :], bo[:, :], ALU.add).then_inc(with_bo, 1)
                if first:
                    pool.wait_ge(prep, 3)
                pool.wait_ge(with_bo, TT * M + TT)
                stand_alone(pool, passed)
                for t in range(TT):
                    pool.tensor_scalar(xg[par][:, t, :], xg[par][:, t, :], gate[:, 1, par:par + 1], None, ALU.mult)\
                        .then_inc(kept, 1)
                for t in range(TT):
                    pool.wait_ge(kept, TT * M + t + 1)
                    pool.tensor_tensor(xg[par][:, t, :], xg[par][:, t, :], gb2[:, par, :], ALU.add).then_inc(kept_b, 1)
                pool.wait_ge(veps_done, M + 1)
                pool.tensor_tensor(rstd[:, :], veps[:, :], half[:, :], ALU.pow).then_inc(rstd_done, 1)

            def window(it, par, ahead, load, first=False):
                if ahead:
                    mit, mpar = (it, 1) if par == 0 else (it + 1, 0)
                    chunk(mit, mpar, 2 * it + par + 1)

            chunk(0, 0, 0, first=True)
            run(pool, window)

        @block.scalar
        def _(act):

            def piece_hi(n):
                act.wait_ge(w_loaded[n % STAGES], 16 * (n // STAGES + 1))
                nc.scalar.activation(pieces[n][1][0], staged(n), ACT.Copy).then_inc(w_hi, 1)

            def affine(M, k, first=False):
                act.wait_ge(tr_done, KD * M + k + 1)
                if k >= 2 or not first:
                    act.wait_ge(ht_split, KD * M + k - 1)
                nc.scalar.activation(htf[k % 2][:, :], ps_tr[k % 2][:, 0:T], ACT.Identity,
                                     scale=col[:, C_G2 + k:C_G2 + k + 1],
                                     bias=col[:, C_B2LN + k:C_B2LN + k + 1]).then_inc(htf_done, 1)

            def window(it, par, ahead, load, first=False):
                N = 2 * it + par
                for f in range(KF):
                    if first:
                        for n in pieces_for(f):
                            piece_hi(n)
                    act.wait_ge(h_done, KF * N + f + 1)
                    act.wait_ge(act_split, 2 + KF * N + f - 1)
                    nc.scalar.activation(act_f[f % 2][:, :], ps_h[f % 2][:, 0:T], ACT.Gelu,
                                         bias=col[:, C_MLP_B1 + f:C_MLP_B1 + f + 1]).then_inc(gelu_done, 1)
                    if ahead and f == TURN_AT:
                        for k in range(KD):
                            affine(N + 1, k)

            for n in range(WO_PIECES + 4):
                piece_hi(n)
            act.wait_ge(col_loaded, 16)
            for k in range(KD):
                affine(0, k, first=True)
            for n in range(WO_PIECES + 4, WO_PIECES + 2 * LEAD):
                piece_hi(n)
            run(act, window)

        @block.vector
        def _(dve):
            nc.vector.memset(stats[:, :, :], 0.0).then_inc(act_split, 2)
            nc.vector.memset(mean_var[:, :, :], 0.0).then_inc(y_done, 2)
            dve.wait_ge(act_split, 2)
            dve.wait_ge(y_done, 2)

            def ctx_halves(M):
                dve.wait_ge(ctx_loaded, 16 * M + 16)
                dve.wait_ge(projected, TT * M)
                nc.vector.tensor_copy(cts[0][:, :, :], cf[:, :, :]).then_inc(ctx_hi, 1)
                dve.wait_ge(ctx_hi, M + 1)
                nc.vector.tensor_tensor(cts[1][:, :, :], cf[:, :, :], cts[0][:, :, :].bitcast(F32), ALU.subtract)\
                  .then_inc(ctx_split, 1)

            def piece_lo(n):
                dve.wait_ge(w_hi, n + 1)
                nc.vector.tensor_tensor(pieces[n][1][1], staged(n), pieces[n][1][0].bitcast(F32), ALU.subtract)\
                  .then_inc(w_split, 1)

            ctx_halves(0)
            for n in range(WO_PIECES):
                piece_lo(n)
            dve.wait_ge(small_loaded, 48)
            nc.vector.tensor_scalar(gate[:, 1, :], gate[:, 0, :], -1.0, 1.0, ALU.mult, ALU.add).then_inc(prep, 1)
            for b in range(BATCH):
                nc.vector.tensor_scalar(gb2[:, b, :], gb2[:, b, :], gate[:, 0, b:b + 1], None, ALU.mult).then_inc(prep, 1)

            def residual(M, t):
                dve.wait_ge(projected, TT * M + t + 1)
                dve.wait_ge(with_bo, TT * M + TT)
                nc.vector.tensor_tensor(x1[:, t, :], ps_p[t][:, :], x1[:, t, :], ALU.add).then_inc(x1_done, 1)

            def statistics(M, t):
                dve.wait_ge(x1_done, TT * M + t + 1)
                nc.vector.bn_stats(stats[:, t, :], x1[:, t, :]).then_inc(stats_done, 1)

            def variance(M):
                dve.wait_ge(stats_done, TT * M + TT)
                stand_alone(dve, passed)
                for t in range(TT):
                    nc.vector.bn_aggr(mean_var[:, t, :], stats[:, t, :]).then_inc(aggr_done, 1)
                dve.wait_ge(aggr_done, TT * M + TT)
                nc.vector.tensor_scalar(veps[:, :], mean_var[:, :, 1], EPS, None, ALU.add).then_inc(veps_done, 1)

            def keep(M, par, t):
                dve.wait_ge(kept_b, TT * M + t + 1)
                nc.vector.scalar_tensor_tensor(out=xg[par][:, t, :], in0=x1[:, t, :], scalar=gate[:, 0, par:par + 1],
                                               in1=xg[par][:, t, :], op0=ALU.mult, op1=ALU.add).then_inc(z_done, 1)

            def normalise(M, t):
                dve.wait_ge(rstd_done, M + 1)
                dve.wait_ge(z_done, TT * M + t + 1)
                nc.vector.tensor_scalar(x1[:, t, :], x1[:, t, :], mean_var[:, t, 0:1], rstd[:, t:t + 1],
                                        ALU.subtract, ALU.mult).then_inc(nrm_done, 1)

            def h_split(M, par, k):
                dve.wait_ge(htf_done, KD * M + k + 1)
                nc.vector.tensor_copy(hts[par][0][:, k, :], htf[k % 2][:, :]).then_inc(ht_hi, 1)
                dve.wait_ge(ht_hi, KD * M + k + 1)
                nc.vector.tensor_tensor(hts[par][1][:, k, :], htf[k % 2][:, :],
                                        hts[par][0][:, k, :].bitcast(F32), ALU.subtract).then_inc(ht_split, 1)

            for t in range(TT):
                residual(0, t)
                statistics(0, t)
            variance(0)
            for n in range(WO_PIECES, WO_PIECES + 2):
                piece_lo(n)
            for t in range(TT):
                keep(0, 0, t)
            for t in range(TT):
                normalise(0, t)
            for n in range(WO_PIECES + 2, WO_PIECES + 4):
                piece_lo(n)
            for k in range(KD):
                h_split(0, 0, k)
            for n in range(WO_PIECES + 4, WO_PIECES + 2 * LEAD):
                piece_lo(n)

            def window(it, par, ahead, load, first=False):
                N = 2 * it + par
                M = N + 1
                mpar = 1 - par

                def gelu_split(f):
                    dve.wait_ge(gelu_done, KF * N + f + 1)
                    dve.wait_ge(y_done, KF * N + f + 1)
                    nc.vector.tensor_copy(acts[f % 2][0][:, :], act_f[f % 2][:, :]).then_inc(act_hi, 1)
                    dve.wait_ge(act_hi, KF * N + f + 1)
                    nc.vector.tensor_tensor(acts[f % 2][1][:, :], act_f[f % 2][:, :],
                                            acts[f % 2][0][:, :].bitcast(F32), ALU.subtract).then_inc(act_split, 1)

                for f in range(KF):
                    if first:
                        for n in pieces_for(f):
                            piece_lo(n)
                    gelu_split(f)
                    if ahead:
                        if f == 1:
                            ctx_halves(M)
                        if PROJECT_AT < f <= PROJECT_AT + TT:
                            residual(M, f - PROJECT_AT - 1)
                            statistics(M, f - PROJECT_AT - 1)
                        if f == PROJECT_AT + TT + 1:
                            variance(M)
                        if f == PROJECT_AT + TT + 2:
                            for t in range(TT):
                                keep(M, mpar, t)
                        if f == PROJECT_AT + TT + 3:
                            for t in range(TT):
                                normalise(M, t)
                        if f == TURN_AT:
                            for k in range(KD):
                                h_split(M, mpar, k)
                for t in range(TT):
                    dve.wait_ge(y_done, 2 + KF * N + KF)
                    nc.vector.scalar_tensor_tensor(out=xg[par][:, t, :], in0=ps_acc[t][:, :],
                                                   scalar=gate[:, 0, par:par + 1], in1=xg[par][:, t, :],
                                                   op0=ALU.mult, op1=ALU.add).then_inc(acc_free, 1)

            run(dve, window)

        @block.tensor
        def _(pe):
            def project_out(M, t, first=False):
                if t == 0:
                    pe.wait_ge(ctx_split, M + 1)
                    pe.wait_ge(x1_done, TT * M)
                for k in range(KD):
                    if first and k % BLOCKS == 0:
                        pe.wait_ge(w_split, k // BLOCKS + 1)
                    last = product3(pe, ps_p[t][:, :], [c[:, k, t * P:(t + 1) * P] for c in cts],
                                    [w[:, k, :] for w in wos], k == 0, k == KD - 1)
                last.then_inc(projected, 1)

            def transposes(M, first=False):
                pe.wait_ge(nrm_done, TT * M + TT)
                for k in range(KD):
                    if k >= 2 or not first:
                        pe.wait_ge(htf_done, KD * M + k - 1)
                    for t in range(TT):
                        last = pe.transpose(ps_tr[k % 2][:, t * P:(t + 1) * P], x1[:, t, k * P:(k + 1) * P], ident[:, :])
                    last.then_inc(tr_done, 1)

            pe.sem_inc(acc_free, 1)
            for t in range(TT):
                project_out(0, t, first=True)
            pe.wait_ge(ident_made, 3)
            transposes(0, first=True)

            def window(it, par, ahead, load, first=False):
                N = 2 * it + par

                def hidden(f):
                    if f == 0:
                        pe.wait_ge(ht_split, KD * N + KD)
                    pe.wait_ge(act_split, 2 + KF * N + f - 1)
                    if first and f % BLOCKS == 0:
                        pe.wait_ge(w_split, WO_PIECES + 2 * (f // BLOCKS) + 1)
                    for k in range(KD):
                        last = product3(pe, ps_h[f % 2][:, 0:T], [w[:, k, f * P:(f + 1) * P] for w in w1s],
                                        [h[:, k, :] for h in hts[par]], k == 0, k == KD - 1)
                    last.then_inc(h_done, 1)

                def output(f):
                    pe.wait_ge(act_split, 2 + KF * N + f + 1)
                    if first and f % BLOCKS == 0:
                        pe.wait_ge(w_split, WO_PIECES + 2 * (f // BLOCKS) + 2)
                    if f == 0:
                        pe.wait_ge(acc_free, TT * N + 1)
                    for t in range(TT):
                        last = product3(pe, ps_acc[t][:, :], [a[:, t * P:(t + 1) * P] for a in acts[f % 2]],
                                        [w[:, f, :] for w in w2s], f == 0, f == KF - 1)
                    last.then_inc(y_done, 1)

                for f in range(KF):
                    hidden(f)
                    if f:
                        output(f - 1)
                    if ahead:
                        if PROJECT_AT <= f < PROJECT_AT + TT:
                            project_out(N + 1, f - PROJECT_AT)
                        if f == TURN_AT:
                            transposes(N + 1)
                output(KF - 1)

            run(pe, window)


def program(nc, x, xt, down_t, up_t, expert_t, cols, rows, ids, gates, wq, wk, wv, wo, w1, w2, out):
    x0_s = nc.dram_tensor("x0_scratch", (TOKENS, D), F32).ap()
    qk_s = nc.dram_tensor("qk_scratch", (2, D, 2, TOKENS), F32).ap()
    v_s = nc.dram_tensor("v_scratch", (TOKENS, D), F32).ap()
    ctx_s = nc.dram_tensor("ctx_scratch", (D, TOKENS), F32).ap()
    project(nc, x, xt, down_t, up_t, expert_t, cols, rows, ids, wq, wk, wv, x0_s, qk_s, v_s)
    attend(nc, qk_s, v_s, ctx_s)
    mlp(nc, ctx_s, x0_s, cols, rows, gates, wo, w1, w2, out)


def kernel(**inputs):
    import numpy as np
    import concourse.bacc as bacc
    from concourse.bass_utils import run_bass_kernel_spmd

    a = {k.replace("_cond", ""): np.asarray(v) for k, v in inputs.items()}
    x = a["x"].reshape(TOKENS, D)

    def column(v):
        return v.reshape(-1, P).T

    cols = np.concatenate([column(a["L0_down_b"]), a["L0_expert_b"].T, a["L0_domain_emb"].T,
                           column(a["L1_bq"]), column(a["L1_bk"]), column(a["L1_gamma1"]), column(a["L1_beta1"]),
                           column(a["L1_gamma2"]), column(a["L1_beta2"]), column(a["L1_b1"])], axis=1)
    rows = np.stack([a["L0_up_b"], a["L0_ln_gamma"], a["L0_ln_beta"], a["L1_bv"], a["L1_bo"], a["L1_b2"]])
    arrays = {
        "x": x, "xt": x.T, "down_t": a["L0_down_W"].T, "up_t": a["L0_up_W"].T,
        "expert_t": a["L0_expert_W"].transpose(2, 0, 1), "cols": cols,
        "rows": np.broadcast_to(rows[None], (P, *rows.shape)),
        "ids": np.broadcast_to(inputs["itok_B_0_15"], (P, BATCH)),
        "gates": np.broadcast_to(inputs["condB_gatescore"], (P, BATCH)),
        "wq": a["L1_Wq"], "wk": a["L1_Wk"], "wv": a["L1_Wv"], "wo": a["L1_Wo"], "w1": a["L1_W1"], "w2": a["L1_W2"],
    }
    arrays = {f"in_{k}": np.ascontiguousarray(v) for k, v in arrays.items()}
    nc = bacc.Bacc("TRN2", target_bir_lowering=False, num_devices=1)
    aps = {k[3:]: nc.dram_tensor(k, v.shape, mybir.dt.from_np(v.dtype), kind="ExternalInput").ap()
           for k, v in arrays.items()}
    out = nc.dram_tensor("out_0", (TOKENS, D), F32, kind="ExternalOutput").ap()
    program(nc, out=out, **aps)
    r = run_bass_kernel_spmd(nc, [arrays], core_ids=[0])
    return r.results[0]["out_0"].reshape(BATCH, SEQ, D)
```
